# Optimizing a Trainium2 kernel written in Bass

```python
import numpy as np
import jax
import jax.numpy as jnp

def _softmax(x, axis=-1):
    return jax.nn.softmax(x, axis=axis)

def _gelu(x):
    return jax.nn.gelu(x, approximate=True)

def _silu(x):
    return jax.nn.silu(x)

def _sigmoid(x):
    return jax.nn.sigmoid(x)

def _layernorm(x, axis=-1, eps=1e-05):
    m = jnp.mean(x, axis=axis, keepdims=True)
    v = jnp.var(x, axis=axis, keepdims=True)
    return (x - m) / jnp.sqrt(v + eps)

def _scatter_add(tgt, idx, src, axis=0):
    return tgt.at[idx].add(src)

def _segment_sum(src, seg, n):
    return jax.ops.segment_sum(src, seg, n)
kernel_name = 'mk_recurrent_d1_jaxref_r8_aba9d5'

def setup_inputs(seed: int=0):
    np.random.seed(seed)
    _w = jnp.asarray

    def _L0_attn_setup():
        import jax, jax.numpy as jnp
        import numpy as np
        DIM = 128
        HEADS = 16
        DIM_HEAD = DIM // HEADS
        LATENT = DIM // 4
        SCALE = DIM_HEAD ** (-0.5)
        key = jax.random.key(seed)
        ks = jax.random.split(key, 8)
        B, S = (2, 256)
        init = lambda k, shape, fan_in: jax.random.normal(k, shape, jnp.float32) * fan_in ** (-0.5)
        return {'x': jax.random.normal(ks[0], (B, S, DIM), jnp.float32), 'Wq': init(ks[1], (DIM, DIM), DIM), 'bq': jnp.zeros((DIM,), jnp.float32), 'Wl': init(ks[2], (DIM, LATENT), DIM), 'bl': jnp.zeros((LATENT,), jnp.float32), 'Wk': init(ks[3], (LATENT, DIM), LATENT), 'bk': jnp.zeros((DIM,), jnp.float32), 'Wv': init(ks[4], (LATENT, DIM), LATENT), 'bv': jnp.zeros((DIM,), jnp.float32), 'Wo': init(ks[5], (DIM, DIM), DIM), 'bo': jnp.zeros((DIM,), jnp.float32)}
    _L0_attn_in = _L0_attn_setup()

    def _L0_ffn_setup():
        import jax, jax.numpy as jnp
        import numpy as np
        DIM = 128
        DEPTH = 6
        HEADS = 16
        DIM_HEAD = 64
        WINDOW = 32
        INNER = HEADS * DIM_HEAD
        DIM_INNER = int(DIM * 4 * 2 / 3)
        QK_SCALE = 8.0

        def shift_tokens(t):
            a, s = jnp.split(t, 2, -1)
            s = jnp.pad(s, ((0, 0), (1, 0), (0, 0)))[:, :-1]
            return jnp.concatenate([a, s], -1)

        def l2norm(t):
            return t / jnp.maximum(jnp.linalg.norm(t, axis=-1, keepdims=True), 1e-12)

        def rotate_half(x):
            x1, x2 = jnp.split(x, 2, -1)
            return jnp.concatenate([-x2, x1], -1)

        def rotary_tables(n):
            half = jnp.arange(0, DIM_HEAD, 2, dtype=jnp.float32)
            inv_freq = 1.0 / 10000.0 ** (half / DIM_HEAD)
            t = jnp.arange(n, dtype=jnp.float32)
            freqs = t[:, None] * inv_freq[None, :]
            freqs = jnp.concatenate([freqs, freqs], -1)
            base_scale = (half + 0.4 * DIM_HEAD) / (1.4 * DIM_HEAD)
            power = (t - n // 2) / (WINDOW // 2)
            scale = base_scale[None, :] ** power[:, None]
            scale = jnp.concatenate([scale, scale], -1)
            return (freqs, scale)

        def local_attention(q, k, v):
            b, h, n, d = q.shape
            w = WINDOW
            nw = n // w
            bq = q.reshape(b, h, nw, w, d)
            bk = k.reshape(b, h, nw, w, d)
            bv = v.reshape(b, h, nw, w, d)

            def look(t):
                p = jnp.pad(t, ((0, 0), (0, 0), (1, 0), (0, 0), (0, 0)))
                return jnp.concatenate([p[:, :, :nw], p[:, :, 1:]], axis=3)
            bk2, bv2 = (look(bk), look(bv))
            seq = jnp.arange(n).reshape(nw, w)
            seq_p = jnp.pad(seq, ((1, 0), (0, 0)), constant_values=-1)
            jt = jnp.concatenate([seq_p[:nw], seq_p[1:]], axis=1)
            it = seq[:, :, None]
            jb = jt[:, None, :]
            mask = (it < jb) | (it > jb + w) | (jb == -1)
            sim = jnp.einsum('bhwie,bhwje->bhwij', bq, bk2) * QK_SCALE
            sim = jnp.where(mask, -jnp.finfo(sim.dtype).max, sim)
            attn = jax.nn.softmax(sim, -1)
            out = jnp.einsum('bhwij,bhwje->bhwie', attn, bv2)
            return out.reshape(b, h, n, d)

        def attn_layer(x, Wqkv, qs, ksc, Wo):
            b, n, _ = x.shape
            qkv = x @ Wqkv
            q, k, v = jnp.split(qkv, 3, -1)
            sh = lambda t: t.reshape(b, n, HEADS, DIM_HEAD).transpose(0, 2, 1, 3)
            q, k, v = (sh(q), sh(k), sh(v))
            q = l2norm(q) * qs
            k = l2norm(k) * ksc
            freqs, scale = rotary_tables(n)
            cos, sin = (jnp.cos(freqs), jnp.sin(freqs))
            q = q * cos * scale + rotate_half(q) * sin * scale
            inv = 1.0 / scale
            k = k * cos * inv + rotate_half(k) * sin * inv
            out = local_attention(q, k, v)
            out = out.transpose(0, 2, 1, 3).reshape(b, n, INNER)
            return out @ Wo

        def ffn_layer(x, g, bln, W1, b1, W2, b2):
            mu = x.mean(-1, keepdims=True)
            var = ((x - mu) ** 2).mean(-1, keepdims=True)
            xn = (x - mu) / jnp.sqrt(var + 1e-05) * g + bln
            hg = xn @ W1 + b1
            a, gate = jnp.split(hg, 2, -1)
            return a * jax.nn.gelu(gate, approximate=False) @ W2 + b2
        key = jax.random.key(seed)
        ks = jax.random.split(key, 8)
        B, N = (2, 256)
        init = lambda k, shape: jax.random.normal(k, shape, jnp.float32) * 0.02
        return {'x': jax.random.normal(ks[0], (B, N, DIM), jnp.float32), 'Wqkv': init(ks[1], (DEPTH, DIM, 3 * INNER)), 'q_scale': jnp.ones((DEPTH, DIM_HEAD), jnp.float32), 'k_scale': jnp.ones((DEPTH, DIM_HEAD), jnp.float32), 'Wo': init(ks[2], (DEPTH, INNER, DIM)), 'ln_g': jnp.ones((DEPTH, DIM), jnp.float32), 'ln_b': jnp.zeros((DEPTH, DIM), jnp.float32), 'W1': init(ks[3], (DEPTH, DIM, 2 * DIM_INNER)), 'b1': jnp.zeros((DEPTH, 2 * DIM_INNER), jnp.float32), 'W2': init(ks[4], (DEPTH, DIM_INNER, DIM)), 'b2': jnp.zeros((DEPTH, DIM), jnp.float32)}
    _L0_ffn_in = _L0_ffn_setup()
    _d = {'L0_attn_x': _L0_attn_in['x'], 'L0_attn_Wq': _L0_attn_in['Wq'], 'L0_attn_bq': _L0_attn_in['bq'], 'L0_attn_Wl': _L0_attn_in['Wl'], 'L0_attn_bl': _L0_attn_in['bl'], 'L0_attn_Wk': _L0_attn_in['Wk'], 'L0_attn_bk': _L0_attn_in['bk'], 'L0_attn_Wv': _L0_attn_in['Wv'], 'L0_attn_bv': _L0_attn_in['bv'], 'L0_attn_Wo': _L0_attn_in['Wo'], 'L0_attn_bo': _L0_attn_in['bo'], 'L0_ffn_Wqkv': _L0_ffn_in['Wqkv'], 'L0_ffn_q_scale': _L0_ffn_in['q_scale'], 'L0_ffn_k_scale': _L0_ffn_in['k_scale'], 'L0_ffn_Wo': _L0_ffn_in['Wo'], 'L0_ffn_ln_g': _L0_ffn_in['ln_g'], 'L0_ffn_ln_b': _L0_ffn_in['ln_b'], 'L0_ffn_W1': _L0_ffn_in['W1'], 'L0_ffn_b1': _L0_ffn_in['b1'], 'L0_ffn_W2': _L0_ffn_in['W2'], 'L0_ffn_b2': _L0_ffn_in['b2']}
    _x0 = _d['L0_attn_x']
    _d['L0_attn_x'] = jax.random.normal(jax.random.fold_in(jax.random.key(seed), 1), (4, 512, 128), dtype=_x0.dtype)
    del _x0
    return _d

def reference(L0_attn_x, L0_attn_Wq, L0_attn_bq, L0_attn_Wl, L0_attn_bl, L0_attn_Wk, L0_attn_bk, L0_attn_Wv, L0_attn_bv, L0_attn_Wo, L0_attn_bo, L0_ffn_Wqkv, L0_ffn_q_scale, L0_ffn_k_scale, L0_ffn_Wo, L0_ffn_ln_g, L0_ffn_ln_b, L0_ffn_W1, L0_ffn_b1, L0_ffn_W2, L0_ffn_b2):

    def _L0_attn_ref(x, Wq, bq, Wl, bl, Wk, bk, Wv, bv, Wo, bo):
        import jax, jax.numpy as jnp
        import numpy as np
        DIM = 128
        HEADS = 16
        DIM_HEAD = DIM // HEADS
        LATENT = DIM // 4
        SCALE = DIM_HEAD ** (-0.5)
        B, S, D = x.shape
        H, Dh = (HEADS, DIM_HEAD)
        q = (x @ Wq + bq).reshape(B, S, H, Dh)
        latent = x @ Wl + bl
        k = (latent @ Wk + bk).reshape(B, S, H, Dh)
        v = (latent @ Wv + bv).reshape(B, S, H, Dh)
        scores = jnp.einsum('bihd,bjhd->bhij', q, k) * SCALE
        attn = jax.nn.softmax(scores, axis=-1)
        out = jnp.einsum('bhij,bjhd->bihd', attn, v).reshape(B, S, D)
        out = out @ Wo + bo
        return out

    def _L0_ffn_ref(x, Wqkv, q_scale, k_scale, Wo, ln_g, ln_b, W1, b1, W2, b2):
        import jax, jax.numpy as jnp
        import numpy as np
        DIM = 128
        DEPTH = 6
        HEADS = 16
        DIM_HEAD = 64
        WINDOW = 32
        INNER = HEADS * DIM_HEAD
        DIM_INNER = int(DIM * 4 * 2 / 3)
        QK_SCALE = 8.0

        def shift_tokens(t):
            a, s = jnp.split(t, 2, -1)
            s = jnp.pad(s, ((0, 0), (1, 0), (0, 0)))[:, :-1]
            return jnp.concatenate([a, s], -1)

        def l2norm(t):
            return t / jnp.maximum(jnp.linalg.norm(t, axis=-1, keepdims=True), 1e-12)

        def rotate_half(x):
            x1, x2 = jnp.split(x, 2, -1)
            return jnp.concatenate([-x2, x1], -1)

        def rotary_tables(n):
            half = jnp.arange(0, DIM_HEAD, 2, dtype=jnp.float32)
            inv_freq = 1.0 / 10000.0 ** (half / DIM_HEAD)
            t = jnp.arange(n, dtype=jnp.float32)
            freqs = t[:, None] * inv_freq[None, :]
            freqs = jnp.concatenate([freqs, freqs], -1)
            base_scale = (half + 0.4 * DIM_HEAD) / (1.4 * DIM_HEAD)
            power = (t - n // 2) / (WINDOW // 2)
            scale = base_scale[None, :] ** power[:, None]
            scale = jnp.concatenate([scale, scale], -1)
            return (freqs, scale)

        def local_attention(q, k, v):
            b, h, n, d = q.shape
            w = WINDOW
            nw = n // w
            bq = q.reshape(b, h, nw, w, d)
            bk = k.reshape(b, h, nw, w, d)
            bv = v.reshape(b, h, nw, w, d)

            def look(t):
                p = jnp.pad(t, ((0, 0), (0, 0), (1, 0), (0, 0), (0, 0)))
                return jnp.concatenate([p[:, :, :nw], p[:, :, 1:]], axis=3)
            bk2, bv2 = (look(bk), look(bv))
            seq = jnp.arange(n).reshape(nw, w)
            seq_p = jnp.pad(seq, ((1, 0), (0, 0)), constant_values=-1)
            jt = jnp.concatenate([seq_p[:nw], seq_p[1:]], axis=1)
            it = seq[:, :, None]
            jb = jt[:, None, :]
            mask = (it < jb) | (it > jb + w) | (jb == -1)
            sim = jnp.einsum('bhwie,bhwje->bhwij', bq, bk2) * QK_SCALE
            sim = jnp.where(mask, -jnp.finfo(sim.dtype).max, sim)
            attn = jax.nn.softmax(sim, -1)
            out = jnp.einsum('bhwij,bhwje->bhwie', attn, bv2)
            return out.reshape(b, h, n, d)

        def attn_layer(x, Wqkv, qs, ksc, Wo):
            b, n, _ = x.shape
            qkv = x @ Wqkv
            q, k, v = jnp.split(qkv, 3, -1)
            sh = lambda t: t.reshape(b, n, HEADS, DIM_HEAD).transpose(0, 2, 1, 3)
            q, k, v = (sh(q), sh(k), sh(v))
            q = l2norm(q) * qs
            k = l2norm(k) * ksc
            freqs, scale = rotary_tables(n)
            cos, sin = (jnp.cos(freqs), jnp.sin(freqs))
            q = q * cos * scale + rotate_half(q) * sin * scale
            inv = 1.0 / scale
            k = k * cos * inv + rotate_half(k) * sin * inv
            out = local_attention(q, k, v)
            out = out.transpose(0, 2, 1, 3).reshape(b, n, INNER)
            return out @ Wo

        def ffn_layer(x, g, bln, W1, b1, W2, b2):
            mu = x.mean(-1, keepdims=True)
            var = ((x - mu) ** 2).mean(-1, keepdims=True)
            xn = (x - mu) / jnp.sqrt(var + 1e-05) * g + bln
            hg = xn @ W1 + b1
            a, gate = jnp.split(hg, 2, -1)
            return a * jax.nn.gelu(gate, approximate=False) @ W2 + b2
        for i in range(DEPTH):
            x = attn_layer(shift_tokens(x), Wqkv[i], q_scale[i], k_scale[i], Wo[i]) + x
            x = ffn_layer(shift_tokens(x), ln_g[i], ln_b[i], W1[i], b1[i], W2[i], b2[i]) + x
        return x
    x = L0_attn_x
    xn = _layernorm(x, axis=-1)
    s = _L0_attn_ref(xn, L0_attn_Wq, L0_attn_bq, L0_attn_Wl, L0_attn_bl, L0_attn_Wk, L0_attn_bk, L0_attn_Wv, L0_attn_bv, L0_attn_Wo, L0_attn_bo)
    g = _silu(_L0_ffn_ref(xn, L0_ffn_Wqkv, L0_ffn_q_scale, L0_ffn_k_scale, L0_ffn_Wo, L0_ffn_ln_g, L0_ffn_ln_b, L0_ffn_W1, L0_ffn_b1, L0_ffn_W2, L0_ffn_b2))
    x = x + s * g
    return x

_drawn_inputs = setup_inputs


def setup_inputs(seed=0):
    import zlib

    import numpy as np

    out = dict(_drawn_inputs(seed))
    spreads = {'L0_attn_bq': (0.0, 0.8),
     'L0_attn_bl': (0.0, 0.1),
     'L0_attn_bk': (0.0, 2.0),
     'L0_attn_bv': (0.0, 0.1),
     'L0_attn_bo': (0.0, 0.1),
     'L0_ffn_q_scale': (1.0, 0.6),
     'L0_ffn_k_scale': (1.0, 0.6),
     'L0_ffn_ln_g': (1.0, 0.6),
     'L0_ffn_ln_b': (0.0, 0.8),
     'L0_ffn_b1': (0.0, 0.8),
     'L0_ffn_b2': (0.0, 0.398)}
    factors = {'L0_ffn_Wqkv': 3.111, 'L0_ffn_Wo': 3.14, 'L0_ffn_W1': 8.0, 'L0_ffn_W2': 8.0}
    for name, (base, spread) in spreads.items():
        noise = np.random.default_rng([zlib.crc32(name.encode()), seed]).standard_normal(out[name].shape)
        drawn = base * np.exp(spread * noise) if base else spread * noise
        out[name] = jnp.asarray(drawn.astype(out[name].dtype))
    for name, factor in factors.items():
        out[name] = (out[name] * factor).astype(out[name].dtype)
    return out
```

```python
import concourse.bass as bass
from concourse import mybir
from contextlib import ExitStack
import numpy as np

B, S, D = 4, 512, 128
T = B * S
NT = T // 128
H = 16
DH = D // H
LAT = D // 4
DEPTH = 6
HD = 64
INNER = H * HD
PAIRS = INNER // 128
W = 32
NW = S // W
HID = int(D * 4 * 2 / 3)
HT = HID // 128
TAIL = HID - HT * 128
HN = HT + 1
NU = B * HN
NPAR = 5 + 2 * HN
NEG = -1e30


def gated_stack_kernel(nc, x, wq0, wl0, wk0, wv0, vec0, wog0, qkv, wo, par, w1, w2,
                       rot, mask, const, out):
    f32, bf16 = mybir.dt.float32, mybir.dt.bfloat16
    ALU, ACT, AX = mybir.AluOpType, mybir.ActivationFunctionType, mybir.AxisListType
    ds = bass.ds

    ctx = ExitStack()
    with ctx:
        def sb(name, shape, dt=f32):
            return ctx.enter_context(nc.sbuf_tensor(name, shape, dt))

        def sem(name):
            return ctx.enter_context(nc.semaphore(name))

        x_tok = sb("x_tok", [128, NT, D])
        xT = sb("xT", [128, T])
        sT = sb("sT", [128, T])
        xs = sb("xs", [128, B, S])
        rot_sb = sb("rot_sb", [128, 4, S])
        mask_sb = sb("mask_sb", [128, 1024], bf16)
        const_sb = sb("const_sb", [128, 608])
        identb = sb("identb", [128, 128], bf16)
        ident = const_sb[:, 0:128]
        centre = const_sb[:, 128:256]
        pickrow = const_sb[:, 256:384]
        pickden = const_sb[:, 384:512]
        headsum = const_sb[:, 512:576].rearrange("p (a m) -> p a m", a=2)
        mean128 = const_sb[:, 576:608]
        slab = sb("slab", [128, 3, 128])
        wo_sb = sb("wo_sb", [128, 128])
        par_all = sb("par_all", [128, DEPTH * NPAR])
        par_sb = sb("par_sb", [128, NPAR])
        w1_sb = sb("w1_sb", [128, 2 * HID])
        w2_sb = sb("w2_sb", [128, HN, 128])
        big = sb("big", [128, 15 * T])

        def region(n, k=1):
            return big[:, n * T:(n + k) * T]

        qE, kE, uq, uk, xsw, qr, kr, sqq, sqk, M, P, oT = (region(n) for n in range(12))
        V = [region(12).rearrange("p (w c) -> p w c", c=128), region(13).rearrange("p (w c) -> p w c", c=128)]
        xsw = xsw.rearrange("p (w c) -> p w c", c=128)
        Mv = M.rearrange("p (h w c) -> p h w c", h=2, c=64)
        Pv = P.rearrange("p (h w c) -> p h w c", h=2, c=64)
        rq_row = sb("rq_row", [128, 2, NW + 1, W])
        mx_row = sb("mx_row", [128, 2, NW + 1, W])
        dn_row = sb("dn_row", [128, 2, NW + 1, W])
        ss_t = sb("ss_t", [128, NW, 32])
        rn = sb("rn", [128, 4, NW])
        SKEW = NW + 2
        red = sb("red", [128, 2, 2 * SKEW])
        rsum = sb("rsum", [128, 2, 2 * SKEW])
        rk8 = sb("rk8", [128, 2, NW])
        mx = sb("mx", [128, 2, NW])
        dn = sb("dn", [128, 2, NW])
        rd = sb("rd", [128, 2, NW])
        xc, xsq, xn = region(0), region(1), region(2)
        gel = region(4).rearrange("p (s t) -> p s t", s=4)
        hid = region(7, 2)[:, 0:2 * HN * 512].rearrange("p (a j t) -> p a j t", a=2, j=HN)
        rstd_sb = region(10)[:, 0:512]
        x_n = region(10).rearrange("p (n d) -> p n d", d=D)
        gate, fin = region(0), region(1)
        mask_f = region(11)[:, 0:1024]
        qst = region(0, 2).bitcast(bf16).rearrange("p (h t) -> p h t", h=H)
        kst = region(2, 2).bitcast(bf16).rearrange("p (h t) -> p h t", h=H)
        PT = region(4, 8).rearrange("p (a c k t) -> p a c k t", a=2, c=4, k=4)
        V32 = region(12).rearrange("p (k h c) -> p k h c", k=4, c=32)
        l0 = region(13, 2)
        qf, kf, raw, rden = (l0[:, 512 * n:512 * n + 512] for n in range(4))
        onorm = region(14).rearrange("p (g t) -> p g t", g=4)
        pieces = sb("pieces", [128, 2, 3, 512], bf16)
        latA = sb("latA", [64, 512])
        mx0 = sb("mx0", [128, H, 4])
        mneg = sb("mneg", [128, 4, H])
        mpc = sb("mpc", [128, 4, 3, H], bf16)
        mrows = sb("mrows", [48, 512], bf16)
        st6 = sb("st6", [128, NT, 6])
        mv = sb("mv", [128, NT, 2])
        rstd0, var0, var0t = sb("rstd0", [128, NT]), sb("var0", [128, NT]), sb("var0t", [128, NT])
        ssg, ssw = sb("ssg", [128, 4, NW]), sb("ssw", [128, 4 * NW])
        varw = sb("varw", [128, NT, 32])
        wl0_sb = sb("wl0_sb", [128, LAT])
        wk0_sb = sb("wk0_sb", [LAT, 128])
        wv0_sb = sb("wv0_sb", [LAT + 1, 128])
        vec0_sb = sb("vec0_sb", [128, 4])
        wog_sb = sb("wog_sb", [128, 4, 128])
        wq0_sb = sb("wq0_sb", [128, 128])
        scratch = nc.dram_tensor("piece_scratch", [2, 3, 128, 512], bf16, kind="Internal").ap()

        X = ctx.enter_context(nc.psum_tensor("X", [128, 2048], f32))
        Y = ctx.enter_context(nc.psum_tensor("Y", [128, 2048], f32))

        def pairs(t, h):
            a = t[:, h]
            return bass.AP(a.tensor, a.offset, [list(a.ap[0]), [W, NW], [1, 2 * W]])

        def bank(t, n, k=1):
            return t[:, 512 * n:512 * (n + k)]

        ld_x, ld_c, ld_w0 = [sem(f"ld_x{q}") for q in range(4)], sem("ld_c"), sem("ld_w0")
        init_v, init_p = sem("init_v"), sem("init_p")
        i_var, i_rstd, i_xn, i_tr, i_xT = (sem(n) for n in ("i_var", "i_rstd", "i_xn", "i_tr", "i_xT"))
        dv = sem("dv")
        a_q, a_lat, a_latA, a_kv, a_pc, a_v = (sem(n) for n in ("a_q", "a_lat", "a_latA", "a_kv", "a_pc", "a_v"))
        a_scr, a_st, a_s, a_mx, a_mp, a_mt, a_mr, a_mrow = (
            sem(n) for n in ("a_scr", "a_st", "a_s", "a_mx", "a_mp", "a_mt", "a_mr", "a_mrow"))
        a_sT, a_exp, a_pv, a_raw, a_den, a_rec, a_on, a_acc, a_out = (
            sem(n) for n in ("a_sT", "a_exp", "a_pv", "a_raw", "a_den", "a_rec", "a_on", "a_acc", "a_out"))
        ld_qkv, ld_wo = sem("ld_qkv"), sem("ld_wo")
        xs_ok, xsw_ok, par_ok = sem("xs_ok"), sem("xsw_ok"), sem("par_ok")
        p_mm, p_ev = sem("p_mm"), sem("p_ev")
        v_mm, v_ev = sem("v_mm"), sem("v_ev")
        ss_mm, ss_tr, rn_ok, rq_ok, m_ok = (sem(n) for n in ("ss_mm", "ss_tr", "rn_ok", "rq_ok", "m_ok"))
        u_ok, c_ok, sh_ok, r_ok = (sem(n) for n in ("u_ok", "c_ok", "sh_ok", "r_ok"))
        s_mm, s_rd, s_sub, e_ok, d_ok, pn_ok = (sem(n) for n in ("s_mm", "s_rd", "s_sub", "e_ok", "d_ok", "pn_ok"))
        o_mm, o_ev, y_mm, y_add = (sem(n) for n in ("o_mm", "o_ev", "y_mm", "y_add"))
        ld_w = sem("ld_w")
        c_mm, c_ev, var_mm, var_ev, rs_ok, rb_mm, t_ok, xn_ok = (
            sem(n) for n in ("c_mm", "c_ev", "var_mm", "var_ev", "rs_ok", "rb_mm", "t_ok", "xn_ok"))
        h_mm, g_ok, h_ok, z_mm, z_add = (sem(n) for n in ("h_mm", "g_ok", "h_ok", "z_mm", "z_add"))
        f_g, f_p, f_tr, f_o, st = (sem(n) for n in ("f_g", "f_p", "f_tr", "f_o", "st"))
        rs, vr = sem("rs"), sem("vr")
        sm, lo, po = sem("sm"), sem("lo"), sem("po")

        passed = sem("passed")
        block = ctx.enter_context(nc.Block())

        def stand(eng):
            eng.sem_inc(passed, 1)


        @block.sync
        def _(sp):
            xv = x.rearrange("(n p) d -> p n d", p=128)
            for q in range(4):
                sp.dma_start(x_tok[:, 4 * q:4 * q + 4, :], xv[:, 4 * q:4 * q + 4, :]).then_inc(ld_x[q], 16)
            sp.dma_start(const_sb[:], const).then_inc(ld_c, 16)
            for dst, src in ((wq0_sb, wq0), (wl0_sb, wl0), (wk0_sb, wk0), (wv0_sb, wv0), (vec0_sb, vec0)):
                sp.dma_start(dst[:], src).then_inc(ld_w0, 16)
            sp.dma_start(wog_sb[:], wog0.rearrange("p (g m) -> p g m", g=4)).then_inc(ld_w0, 16)
            sp.dma_start(rot_sb[:], rot.rearrange("p (a t) -> p a t", a=4)).then_inc(ld_c, 16)
            sp.dma_start(mask_f, mask).then_inc(ld_c, 16)
            sp.dma_start(par_all[:], par).then_inc(ld_c, 16)
            sp.dma_start(slab[:], qkv[0]).then_inc(ld_qkv, 16)
            sp.dma_start(wo_sb[:], wo[0]).then_inc(ld_wo, 16)
            sp.dma_start(w1_sb[:], w1[0]).then_inc(ld_w, 16)
            sp.dma_start(w2_sb[:, 0:HT, :], w2[0, 0:HT * 128].rearrange("(j p) n -> p j n", p=128)).then_inc(ld_w, 16)
            sp.dma_start(w2_sb[0:TAIL, HT, :], w2[0, HT * 128:HID]).then_inc(ld_w, 16)
            sp.wait_ge(init_p, 6)
            with sp.Fori(0, B) as b:
                for t in range(2):
                    sp.wait_ge(a_pc, 2 * b + 1 + t)
                    sp.dma_start(scratch[t].rearrange("c p t -> p c t"), pieces[:, t]).then_inc(a_scr, 16)
                sp.wait_ge(a_scr, 32 * b + 32)
                stand(sp)
                sp.wait_ge(a_sT, 32 * b + 1)
                for c in range(3):
                    for p in range(3):
                        sp.dma_start(qst[24 * p + 8 * c:24 * p + 8 * c + 8, :, :],
                                     scratch[0, p].rearrange("(r h) t -> r h t", h=H)).then_inc(a_st, 16)
                for c in range(3):
                    sp.dma_start(kst[24 * c:24 * c + 24, :, :],
                                 scratch[1].rearrange("c (r h) t -> (c r) h t", h=H)).then_inc(a_st, 16)
                sp.wait_ge(a_mr, b + 1)
                for p in range(3):
                    sp.dma_start(qst[96 + p:97 + p, :, :], mrows[16 * p:16 * p + 16, :]).then_inc(a_mrow, 16)

            def next_pair(it):
                sp.wait_ge(v_mm, 4 * it + 4)
                stand(sp)
                sp.dma_start(slab[:], qkv[it + 1]).then_inc(ld_qkv, 16)
                sp.wait_ge(y_mm, 4 * it + 4)
                stand(sp)
                sp.dma_start(wo_sb[:], wo[it + 1]).then_inc(ld_wo, 16)

            with sp.Fori(0, DEPTH - 1) as L:
                with sp.Fori(0, PAIRS) as hp:
                    next_pair(L * PAIRS + hp)
                sp.wait_ge(z_mm, 4 * L + 4)
                stand(sp)
                sp.dma_start(w1_sb[:], w1[L + 1]).then_inc(ld_w, 16)
                sp.dma_start(w2_sb[:, 0:HT, :],
                             w2[L + 1, 0:HT * 128].rearrange("(j p) n -> p j n", p=128)).then_inc(ld_w, 16)
                sp.dma_start(w2_sb[0:TAIL, HT, :], w2[L + 1, HT * 128:HID]).then_inc(ld_w, 16)
            with sp.Fori(0, PAIRS - 1) as hp:
                next_pair((DEPTH - 1) * PAIRS + hp)
            ov = out.rearrange("(n p) d -> p n d", p=128)
            for q in range(4):
                sp.wait_ge(f_o, q + 1)
                sp.dma_start(ov[:, 4 * q:4 * q + 4, :], x_tok[:, 4 * q:4 * q + 4, :]).then_inc(st, 16)
            sp.wait_ge(st, 64)

        @block.tensor
        def _(pe):
            def mm(o, l, r, start=True, stop=True, **k):
                return pe.matmul(o, l, r, start=start, stop=stop, **k)

            pe.wait_ge(ld_c, 64)
            pe.wait_ge(init_v, 7)
            for n in range(NT):
                pe.wait_ge(i_xn, n + 1)
                pe.transpose(Y[:, n * 128:n * 128 + 128], x_n[:, n, :], ident).then_inc(i_tr, 1)

            pe.wait_ge(ld_w0, 96)
            pe.wait_ge(i_xT, 4)
            pe.sem_inc(a_sT, 1)
            pe.sem_inc(s_mm, 2)
            pe.sem_inc(o_mm, 1)
            with pe.Fori(0, B) as b:
                xb = xT[:, ds(b * S, S)]
                pe.wait_ge(a_out, b + 1)
                mm(bank(Y, 0), wq0_sb[:], xb).then_inc(a_q, 1)
                mm(bank(Y, 1)[0:LAT], wl0_sb[:], xb).then_inc(a_lat, 1)
                pe.wait_ge(a_latA, b + 1)
                mm(bank(Y, 2), wk0_sb[:], latA[0:LAT, :])
                for k in range(4):
                    i = mm(bank(Y, 3)[:, 128 * k:128 * k + 128], latA[0:LAT + 1, 128 * k:128 * k + 128], wv0_sb[:])
                i.then_inc(a_kv, 1)
                pe.wait_ge(a_v, b + 1)
                pe.wait_ge(a_st, 192 * b + 192)
                for h in range(H):
                    if h >= 2:
                        pe.wait_ge(a_mx, 16 * b + h - 1)
                    for q in range(4):
                        i = mm(bank((X, Y)[h % 2], q), qst[0:72, h, 128 * q:128 * q + 128], kst[0:72, h, :])
                    i.then_inc(a_s, 1)
                pe.wait_ge(a_mp, b + 1)
                stand(pe)
                for q in range(4):
                    i = pe.transpose(bank(X, 0).bitcast(bf16)[0:48, 128 * q:128 * q + 128],
                                     mpc[:, q].rearrange("p c h -> p (c h)"), identb[:])
                i.then_inc(a_mt, 1)
                pe.wait_ge(a_mr, b + 1)
                pe.wait_ge(a_mrow, 48 * b + 48)
                ring = (bank(X, 0, 2), bank(X, 2, 2), bank(Y, 0, 2))

                def pv(g, k):
                    if k == 0:
                        pe.wait_ge(a_exp, 32 * b + 8 * g + 8)
                        if g:
                            pe.wait_ge(a_raw, 4 * b + g)
                    for c in range(4):
                        i = mm(bank(Y, 2)[32 * c:32 * c + 32], V32[:, k, 4 * g + c, :], PT[:, g % 2, c, k, :],
                               start=k == 0, stop=k == 3)
                    if k == 3:
                        i.then_inc(a_pv, 1)

                def den(g):
                    pe.wait_ge(a_raw, 4 * b + g + 1)
                    if g:
                        pe.wait_ge(a_rec, 4 * b + g)
                    mm(bank(Y, 3), pickden, raw).then_inc(a_den, 1)

                for h in range(H):
                    for e in range(2):
                        n = 2 * h + e
                        if n >= 3:
                            pe.wait_ge(a_exp, 32 * b + n - 2)
                        for k in range(2):
                            i = mm(ring[n % 3][:, 512 * k:512 * k + 512],
                                   kst[0:99, h, 128 * (2 * e + k):128 * (2 * e + k) + 128], qst[0:99, h, :])
                        i.then_inc(a_sT, 1)
                    if h >= 4:
                        pv(h // 4 - 1, h % 4)
                        if h % 4 == 1 and h >= 8:
                            den(h // 4 - 2)
                for k in range(4):
                    pv(3, k)
                    if k == 0:
                        den(2)
                den(3)
                for g in range(4):
                    pe.wait_ge(a_on, 4 * b + g + 1)
                    i = mm(bank(Y, 2), wog_sb[:, g, :], onorm[:, g, :], start=g == 0, stop=g == 3)
                i.then_inc(a_acc, 1)

            def project(it):
                pe.wait_ge(ld_qkv, 16 * it + 16)
                for t in range(2):
                    for b in range(B):
                        if t == 0:
                            pe.wait_ge(y_add, 4 * it + (4, 1, 2, 3)[b])
                        else:
                            pe.wait_ge(p_ev, 8 * it + b + 1)
                        mm(bank(Y, b), slab[:, t, :], xs[:, b, :]).then_inc(p_mm, 1)

            def project_v(it):
                for w in range(NW):
                    if w % 4 == 0:
                        pe.wait_ge(p_ev, 8 * it + 5 + w // 4)
                    i = mm(Y[:, 128 * w:128 * w + 128], xsw[:, w, :], slab[:, 2, :])
                    if w % 4 == 3:
                        i.then_inc(v_mm, 1)

            def norms(it):
                pe.wait_ge(v_ev, 4 * it + 1)
                pe.wait_ge(p_ev, 8 * it + 8)
                for t in range(2):
                    for b in range(B):
                        i = mm(bank(Y, 0)[32 * b:32 * b + 32], headsum[:, t, :], (sqq, sqk)[t][:, S * b:S * b + S],
                               start=t == 0, stop=t == 1)
                i.then_inc(ss_mm, 1)

            def scores(it):
                pe.wait_ge(o_ev, 4 * it + 4)
                for n in range(4):
                    mm(bank(X, n), identb[:], mask_sb[:, 512 * (n % 2):512 * (n % 2) + 512])
                pe.wait_ge(r_ok, 2 * it + 2)
                stand(pe)
                for h in range(2):
                    for w in range(NW):
                        n = 2 * W if w < NW - 1 else W
                        for b in range(B):
                            i = mm(X[32 * b:32 * b + 32, 1024 * h + 64 * w:1024 * h + 64 * w + n],
                                   kr[64 * h:64 * h + 64, S * b + W * w:S * b + W * w + W],
                                   qr[64 * h:64 * h + 64, S * b + W * w:S * b + W * w + n],
                                   start=False, stop=True, skip_group_check=True)
                    i.then_inc(s_mm, 1)

            def outputs(it, par):
                pe.wait_ge(s_rd, 2 * it + 2)
                pe.wait_ge(v_ev, 4 * it + 4)
                pe.wait_ge(pn_ok, 2 * it + 2)
                for w in range(NW):
                    n = 2 * W if w < NW - 1 else W
                    for b in range(B):
                        for h in range(2):
                            i = mm(X[64 * h:64 * h + 64, 512 * b + W * w:512 * b + W * w + n],
                                   V[par][32 * b:32 * b + 32, w, 64 * h:64 * h + 64],
                                   Pv[32 * b:32 * b + 32, h, w, 0:n],
                                   start=w == 0, stop=w == NW - 1, skip_group_check=True)
                i.then_inc(o_mm, 1)

            def out_project(it, next_in_bank0):
                pe.wait_ge(ld_wo, 16 * it + 16)
                for n, b in enumerate((1, 2, 3, 0)):
                    pe.wait_ge(o_ev, 4 * it + n + 5)
                    if next_in_bank0:
                        pe.wait_ge(v_ev, 4 * it + 5 + b)
                        if b == 0:
                            pe.wait_ge(ss_tr, it + 2)
                    mm(bank(Y, b), wo_sb[:], oT[:, S * b:S * b + S]).then_inc(y_mm, 1)

            with pe.Fori(0, DEPTH) as L:
                pe.wait_ge(xs_ok, 4 * L + 2)
                project(L * PAIRS)
                pe.wait_ge(xsw_ok, L + 1)
                project_v(L * PAIRS)
                norms(L * PAIRS)
                with pe.Fori(0, PAIRS // 2 - 1) as j:
                    for k in range(2):
                        it = L * PAIRS + j * 2 + k
                        scores(it)
                        pe.wait_ge(ss_tr, it + 1)
                        pe.wait_ge(v_ev, 4 * it + 4)
                        project(it + 1)
                        project_v(it + 1)
                        outputs(it, k)
                        norms(it + 1)
                        out_project(it, True)
                it = L * PAIRS + PAIRS - 2
                scores(it)
                pe.wait_ge(ss_tr, it + 1)
                pe.wait_ge(v_ev, 4 * it + 4)
                project(it + 1)
                project_v(it + 1)
                outputs(it, 0)
                norms(it + 1)
                out_project(it, True)
                it = L * PAIRS + PAIRS - 1
                scores(it)
                outputs(it, 1)
                out_project(it, False)

                pe.wait_ge(xs_ok, 4 * L + 4)
                for b in range(B):
                    mm(bank(Y, b), centre, xs[:, b, :]).then_inc(c_mm, 1)
                pe.wait_ge(o_ev, 4 * PAIRS * L + 4 * PAIRS + 4)
                for b in range(B):
                    pe.wait_ge(c_ev, 4 * L + b + 1)
                    i = mm(bank(X, 0)[32 * b:32 * b + 32], mean128, xsq[:, S * b:S * b + S])
                i.then_inc(var_mm, 1)
                pe.wait_ge(rs_ok, L + 1)
                for b in range(B):
                    mm(bank(Y, b), pickrow[32 * b:32 * b + 32, :], rstd_sb[32 * b:32 * b + 32, :]).then_inc(rb_mm, 1)
                slots = (bank(X, 0, 2), bank(X, 2, 2), bank(Y, 0, 2))
                pe.wait_ge(ld_w, 48 * L + 48)
                pe.wait_ge(t_ok, 4 * L + 4)

                def down(b):
                    if b >= 2:
                        pe.wait_ge(z_add, 4 * L + b + 3)
                    for j in range(HN):
                        pe.wait_ge(h_ok, NU * L + HN * b + j + 1)
                        k = 128 if j < HT else TAIL
                        i = mm(bank(Y, 2 + b % 2), w2_sb[0:k, j, :], hid[0:k, b % 2, j, :], start=j == 0, stop=j == HT)
                    i.then_inc(z_mm, 1)

                for b in range(B):
                    pe.wait_ge(xn_ok, 4 * L + b + 1)
                    for j in range(HN):
                        n = HN * b + j
                        if n >= 3:
                            pe.wait_ge(h_ok, NU * L + n - 2)
                        s = slots[n % 3]
                        m = 128 if j < HT else TAIL
                        mm(s[0:m, 0:512], w1_sb[:, 128 * j:128 * j + m], xn[:, S * b:S * b + S])
                        mm(s[0:m, 512:1024], w1_sb[:, HID + 128 * j:HID + 128 * j + m], xn[:, S * b:S * b + S]).then_inc(h_mm, 1)
                        if j == 1 and b:
                            down(b - 1)
                down(B - 1)

            for n in range(NT):
                pe.wait_ge(f_p, n // 4 + 1)
                i = pe.transpose(X[:, 128 * n:128 * n + 128], fin[:, 128 * n:128 * n + 128], ident)
                if n % 4 == 3:
                    i.then_inc(f_tr, 1)


        @block.scalar
        def _(act):
            def copy(o, i):
                return act.activation(o, i, ACT.Copy)

            act.sem_inc(o_ev, 4)
            act.sem_inc(a_out, 1)
            for q in range(4):
                act.wait_ge(i_tr, 4 * q + 4)
                copy(xT[:, S * q:S * q + S], bank(Y, q)).then_inc(i_xT, 1)

            act.wait_ge(ld_w0, 96)
            act.wait_ge(init_p, 6)
            with act.Fori(0, B) as b:
                act.wait_ge(a_lat, b + 1)
                act.activation(latA[0:LAT, :], bank(Y, 1)[0:LAT], ACT.Identity,
                               bias=vec0_sb[0:LAT, 3:4]).then_inc(a_latA, 1)
                ring = (bank(X, 0, 2), bank(X, 2, 2), bank(Y, 0, 2))
                for h in range(H):
                    if h % 4 == 0 and h >= 8:
                        act.wait_ge(a_pv, 4 * b + h // 4 - 1)
                    for e in range(2):
                        n = 2 * h + e
                        act.wait_ge(a_sT, 32 * b + n + 2)
                        act.activation(PT[:, (h // 4) % 2, h % 4, 2 * e:2 * e + 2, :],
                                       ring[n % 3].rearrange("p (k t) -> p k t", k=2), ACT.Exp).then_inc(a_exp, 1)
                act.wait_ge(a_acc, b + 1)
                act.activation(sT[:, ds(b * S, S)], bank(Y, 2), ACT.Identity, bias=vec0_sb[:, 2:3]).then_inc(a_out, 1)

            def project(it, t, bs):
                for b in bs:
                    act.wait_ge(p_mm, 8 * it + 4 * t + b + 1)
                    act.activation((sqq, sqk)[t][:, S * b:S * b + S], bank(Y, b), ACT.Square)
                    act.activation((qE, kE)[t][:, S * b:S * b + S], bank(Y, b), ACT.Identity,
                                   scale=par_sb[:, t:t + 1]).then_inc(p_ev, 1)

            def project_v(it, par):
                for c in range(4):
                    act.wait_ge(v_mm, 4 * it + c + 1)
                    copy(V[par][:, 4 * c:4 * c + 4, :], bank(Y, c).rearrange("p (w c) -> p w c", c=128)).then_inc(v_ev, 1)

            def exps(it, h):
                act.wait_ge(s_sub, 2 * it + h + 1)
                act.activation(P[:, 1024 * h:1024 * h + 1024], P[:, 1024 * h:1024 * h + 1024], ACT.Exp).then_inc(e_ok, 1)

            def outputs(it):
                act.wait_ge(o_mm, it + 2)
                for b in (1, 2, 3, 0):
                    copy(oT[:, S * b:S * b + S], bank(X, b)).then_inc(o_ev, 1)

            def step(it, par):
                project(it + 1, 0, (0, 1))
                exps(it, 0)
                project(it + 1, 0, (2, 3))
                exps(it, 1)
                project(it + 1, 1, range(B))
                project_v(it + 1, 1 - par)
                outputs(it)

            with act.Fori(0, DEPTH) as L:
                act.wait_ge(z_add, 4 * L + 4)
                copy(xs[0:64, :, :], xT[0:64].rearrange("p (b t) -> p b t", b=B)).then_inc(xs_ok, 1)
                act.wait_ge(par_ok, L + 1)
                project(L * PAIRS, 0, range(B))
                project(L * PAIRS, 1, range(B))
                project_v(L * PAIRS, 0)
                with act.Fori(0, PAIRS // 2 - 1) as j:
                    for k in range(2):
                        step(L * PAIRS + j * 2 + k, k)
                step(L * PAIRS + PAIRS - 2, 0)
                it = L * PAIRS + PAIRS - 1
                exps(it, 0)
                exps(it, 1)
                outputs(it)

                act.wait_ge(y_add, 4 * PAIRS * L + 4 * PAIRS + 8)
                copy(xs[0:64, :, :], xT[0:64].rearrange("p (b t) -> p b t", b=B)).then_inc(xs_ok, 1)
                for b in range(B):
                    act.wait_ge(c_mm, 4 * L + b + 1)
                    act.activation(xsq[:, S * b:S * b + S], bank(Y, b), ACT.Square)
                    act.activation(xc[:, S * b:S * b + S], bank(Y, b), ACT.Identity,
                                   scale=par_sb[:, 2:3]).then_inc(c_ev, 1)
                for b in range(B):
                    act.wait_ge(t_ok, 4 * L + b + 1)
                    act.activation(xn[:, S * b:S * b + S], xn[:, S * b:S * b + S], ACT.Identity,
                                   bias=par_sb[:, 3:4]).then_inc(xn_ok, 1)
                slots = (bank(X, 0, 2), bank(X, 2, 2), bank(Y, 0, 2))
                for n in range(NU):
                    j = n % HN
                    act.wait_ge(h_mm, NU * L + n + 1)
                    if n >= 4:
                        act.wait_ge(h_ok, NU * L + n - 3)
                    m = 128 if j < HT else TAIL
                    act.activation(gel[0:m, n % 4, :], slots[n % 3][0:m, 512:1024], ACT.Gelu,
                                   bias=par_sb[0:m, 5 + HN + j:6 + HN + j]).then_inc(g_ok, 1)

            for b in range(B):
                if b == 0:
                    act.wait_ge(z_add, 4 * DEPTH + 4)
                act.activation(gate[:, S * b:S * b + S], xT[:, S * b:S * b + S], ACT.Silu).then_inc(f_g, 1)

        @block.vector
        def _(v):
            steps = [0]

            def link(ins, s, base):
                steps[0] += 1
                ins.then_inc(s, 1)
                v.wait_ge(s, base + steps[0])

            def bcast(a, n):
                return a.unsqueeze(2).broadcast_to([128, a.shape[1], n])

            def inverse_root(r, a, t, s, base):
                i32 = mybir.dt.int32
                link(v.tensor_scalar(r.bitcast(i32), a.bitcast(i32), -0.5, float(0x5F3759DF), ALU.mult, ALU.add), s, base)
                for _ in range(4):
                    link(v.tensor_tensor(t, r, r, ALU.mult), s, base)
                    link(v.scalar_tensor_tensor(t, t, -0.5, a, ALU.mult, ALU.mult), s, base)
                    link(v.scalar_tensor_tensor(r, t, 1.5, r, ALU.add, ALU.mult), s, base)

            v.sem_inc(y_add, 8)
            v.sem_inc(z_add, 4)
            v.wait_ge(ld_c, 64)
            v.tensor_copy(identb[:], ident).then_inc(init_v, 1)
            v.tensor_copy(mask_sb[:], mask_f).then_inc(init_v, 1)
            v.memset(red[:], NEG).then_inc(init_v, 1)
            v.memset(rsum[:], 0.0).then_inc(init_v, 1)
            v.memset(mx_row[:], 0.0).then_inc(init_v, 1)
            v.memset(dn_row[:], 1.0).then_inc(init_v, 1)
            v.memset(rq_row[:], 1.0).then_inc(init_v, 1)
            for n in range(NT):
                if n % 4 == 0:
                    v.wait_ge(ld_x[n // 4], 16)
                v.bn_stats(st6[:, n, :], x_tok[:, n, :]).then_inc(i_var, 1)
            for n in range(NT):
                v.wait_ge(i_var, n + 1)
                v.bn_aggr(mv[:, n, :], st6[:, n, :]).then_inc(dv, 1)
            v.wait_ge(dv, NT)
            steps[0] = 0
            link(v.tensor_scalar(var0[:], mv[:, :, 1], 1e-5, None, ALU.add), dv, NT)
            inverse_root(rstd0[:], var0[:], var0t[:], dv, NT)
            for n in range(NT):
                v.tensor_scalar(x_n[:, n, :], x_tok[:, n, :], mv[:, n, 0:1], rstd0[:, n:n + 1],
                                ALU.subtract, ALU.mult).then_inc(i_xn, 1)

            v.wait_ge(ld_w0, 96)
            with v.Fori(0, B) as b:
                steps[0] = 0
                base = 17 * b

                def split(t, src):
                    for c in range(3):
                        link(v.tensor_copy(pieces[:, t, c, :], src), lo, base)
                        if c < 2:
                            link(v.tensor_tensor(src, src, pieces[:, t, c, :], ALU.subtract), lo, base)
                v.wait_ge(a_q, b + 1)
                link(v.tensor_scalar(qf, bank(Y, 0), vec0_sb[:, 0:1], float(DH) ** -0.5, ALU.add, ALU.mult), lo, base)
                split(0, qf)
                v.sem_inc(a_pc, 1)
                v.wait_ge(a_kv, b + 1)
                link(v.tensor_scalar(kf, bank(Y, 2), vec0_sb[:, 1:2], None, ALU.add), lo, base)
                split(1, kf)
                v.sem_inc(a_pc, 1)
                v.tensor_copy(V32[:, :, :, 0:DH], bank(Y, 3).rearrange("p (k h c) -> p k h c", k=4, c=DH)).then_inc(a_v, 1)
                for h in range(H):
                    v.wait_ge(a_s, 16 * b + h + 1)
                    v.tensor_reduce(mx0[:, h, :], (X, Y)[h % 2][:, :].rearrange("p (q t) -> p q t", q=4),
                                    AX.X, ALU.max).then_inc(a_mx, 1)
                v.wait_ge(a_mx, 16 * b + 16)
                link(v.tensor_scalar(mneg[:], mx0[:].rearrange("p h q -> p q h"), -1.0, None, ALU.mult), lo, base)
                for c in range(3):
                    i = v.tensor_copy(mpc[:, :, c, :], mneg[:])
                    if c < 2:
                        link(i, lo, base)
                        link(v.tensor_tensor(mneg[:], mneg[:], mpc[:, :, c, :], ALU.subtract), lo, base)
                    else:
                        i.then_inc(a_mp, 1)
                assert steps[0] == 17, steps
                v.wait_ge(a_mt, b + 1)
                v.tensor_copy(mrows[:], bank(X, 0).bitcast(bf16)[0:48, 0:512]).then_inc(a_mr, 1)
                for g in range(4):
                    v.wait_ge(a_pv, 4 * b + g + 1)
                    if g:
                        v.wait_ge(a_on, 4 * b + g)
                    v.tensor_copy(raw, bank(Y, 2)).then_inc(a_raw, 1)
                    v.wait_ge(a_den, 4 * b + g + 1)
                    v.reciprocal(rden, bank(Y, 3)).then_inc(a_rec, 1)

            def softmax_top(it, h):
                Ph, Mh = P[:, 1024 * h:1024 * h + 1024], M[:, 1024 * h:1024 * h + 1024]
                v.wait_ge(s_mm, 2 * it + h + 1 + 2)
                v.wait_ge(m_ok, 2 * it + h + 1)
                v.wait_ge(o_mm, it + 1)
                v.tensor_tensor(Ph, X[:, 1024 * h:1024 * h + 1024], Mh, ALU.mult).then_inc(s_rd, 1)
                v.wait_ge(s_rd, 2 * it + h + 1)
                base = 12 * it
                link(v.tensor_reduce(skew(red, h), Ph.rearrange("p (n c) -> p n c", c=32), AX.X, ALU.max,
                                     apply_transpose=True), sm, base)
                link(v.tensor_tensor(mx[:, h, :], red[:, h, 0:NW], red[:, h, NW + 1:2 * NW + 1], ALU.max), sm, base)
                link(v.transpose(mx_row[:, h, 0:NW, :], bcast(mx[:, h, :], 32)), sm, base)
                v.tensor_tensor(Pv[:, h], Pv[:, h], pairs(mx_row, h), ALU.subtract).then_inc(s_sub, 1)

            def softmax_sums(it, h):
                base = 12 * it
                v.wait_ge(e_ok, 2 * it + h + 1)
                link(v.tensor_reduce(skew(rsum, h), P[:, 1024 * h:1024 * h + 1024].rearrange("p (n c) -> p n c", c=32),
                                     AX.X, ALU.add, apply_transpose=True), sm, base)
                link(v.tensor_tensor(dn[:, h, :], rsum[:, h, 0:NW], rsum[:, h, NW + 1:2 * NW + 1], ALU.add), sm, base)
                link(v.reciprocal(rd[:, h, :], dn[:, h, :]), sm, base)
                v.transpose(dn_row[:, h, 0:NW, :], bcast(rd[:, h, :], 32)).then_inc(d_ok, 1)

            def skew(t, h):
                return t[:, h, :].rearrange("p (s k) -> p k s", s=2)[:, 0:NW, :]

            SWAP = [(i + 16) % 32 for i in range(32)]

            def cos_part(it, t):
                v.wait_ge(p_ev, 8 * it + 4 * t + 4)
                v.wait_ge(s_mm, 2 * it + 2)
                v.tensor_tensor((qr, kr)[t].rearrange("p (b t) -> p b t", b=B),
                                (qE, kE)[t].rearrange("p (b t) -> p b t", b=B),
                                rot_sb[:, 2 * t:2 * t + 1, :].broadcast_to([128, B, S]), ALU.mult).then_inc(c_ok, 1)

            def sin_part(it, t):
                v.wait_ge(u_ok, 2 * it + t + 1)
                stand(v)
                v.stream_shuffle((uq, uk)[t], (uq, uk)[t], SWAP).then_inc(sh_ok, 1)

            def norms(it):
                v.wait_ge(ss_mm, it + 1)
                v.transpose(ss_t[:].rearrange("p w c -> p (w c)"), bank(Y, 0)).then_inc(ss_tr, 1)
                v.wait_ge(ss_tr, it + 1)
                c, base, steps[0] = steps[0], 14 * it, 0
                link(v.tensor_scalar(ssg[:], ss_t[:, :, 0:4].rearrange("p w c -> p c w"), 1e-24, None, ALU.max), rs, base)
                flat = "p c w -> p (c w)"
                inverse_root(rn[:].rearrange(flat), ssg[:].rearrange(flat), ssw[:], rs, base)
                assert steps[0] == 14
                steps[0] = c
                for h in range(2):
                    v.transpose(rq_row[:, h, 0:NW, :], bcast(rn[:, h, :], 32)).then_inc(rq_ok, 1)

            def add_y(it):
                for n, b in enumerate((1, 2, 3, 0)):
                    v.wait_ge(y_mm, 4 * it + n + 1)
                    v.wait_ge(y_add, 4 * it + n + 5)
                    v.tensor_tensor(xT[:, S * b:S * b + S], bank(Y, b), xT[:, S * b:S * b + S], ALU.add).then_inc(y_add, 1)

            def step(it):
                steps[0] = 0
                softmax_top(it, 0)
                softmax_top(it, 1)
                softmax_sums(it, 0)
                softmax_sums(it, 1)
                cos_part(it + 1, 0)
                sin_part(it + 1, 0)
                cos_part(it + 1, 1)
                sin_part(it + 1, 1)
                norms(it + 1)
                add_y(it)
                assert steps[0] == 12

            v.wait_ge(ld_c, 64)
            v.wait_ge(init_p, 6)
            v.wait_ge(i_xT, 4)
            v.wait_ge(a_out, B + 1)
            x4 = xT[:, :].rearrange("p (b t) -> p b t", b=B)
            with v.Fori(0, DEPTH) as L:
                v.wait_ge(z_add, 4 * L + 4)
                v.tensor_copy(par_sb[:], par_all[:, ds(L * NPAR, NPAR)]).then_inc(par_ok, 1)
                v.tensor_copy(xs[64:128, :, 1:S], x4[64:128, :, 0:S - 1]).then_inc(xs_ok, 1)
                v.wait_ge(xs_ok, 4 * L + 2)
                v.tensor_copy(xsw.rearrange("p w (b l) -> p w b l", b=B),
                              xs[:].rearrange("p b (w l) -> p w b l", w=NW)).then_inc(xsw_ok, 1)
                cos_part(L * PAIRS, 0)
                sin_part(L * PAIRS, 0)
                cos_part(L * PAIRS, 1)
                sin_part(L * PAIRS, 1)
                norms(L * PAIRS)
                with v.Fori(0, PAIRS // 2 - 1) as j:
                    for k in range(2):
                        step(L * PAIRS + j * 2 + k)
                step(L * PAIRS + PAIRS - 2)
                steps[0] = 0
                it = L * PAIRS + PAIRS - 1
                softmax_top(it, 0)
                softmax_top(it, 1)
                softmax_sums(it, 0)
                softmax_sums(it, 1)
                add_y(it)

                v.wait_ge(y_add, 4 * PAIRS * L + 4 * PAIRS + 8)
                v.tensor_copy(xs[64:128, :, 1:S], x4[64:128, :, 0:S - 1]).then_inc(xs_ok, 1)
                v.wait_ge(var_mm, L + 1)
                steps[0] = 0
                base = 15 * L
                link(v.transpose(varw[:].rearrange("p w c -> p (w c)"), bank(X, 0)), vr, base)
                link(v.tensor_scalar(var0[:], varw[:, :, 0], 1e-5, None, ALU.add), vr, base)
                inverse_root(rstd0[:], var0[:], var0t[:], vr, base)
                v.transpose(rstd_sb.rearrange("p (w c) -> p w c", c=32), bcast(rstd0[:], 32)).then_inc(rs_ok, 1)
                assert steps[0] == 15
                for b in range(B):
                    v.wait_ge(rb_mm, 4 * L + b + 1)
                    v.tensor_tensor(xn[:, S * b:S * b + S], bank(Y, b), xc[:, S * b:S * b + S], ALU.mult).then_inc(t_ok, 1)
                slots = (bank(X, 0, 2), bank(X, 2, 2), bank(Y, 0, 2))

                def add_z(b):
                    v.wait_ge(z_mm, 4 * L + b + 1)
                    v.scalar_tensor_tensor(xT[:, S * b:S * b + S], bank(Y, 2 + b % 2), par_sb[:, 4:5],
                                           xT[:, S * b:S * b + S], ALU.add, ALU.add).then_inc(z_add, 1)

                for b in range(B):
                    for j in range(HN):
                        n = HN * b + j
                        v.wait_ge(g_ok, NU * L + n + 1)
                        if j == 0 and b >= 2:
                            v.wait_ge(z_mm, 4 * L + b - 1)
                        m = 128 if j < HT else TAIL
                        v.scalar_tensor_tensor(hid[0:m, b % 2, j, :], slots[n % 3][0:m, 0:512], par_sb[0:m, 5 + j:6 + j],
                                               gel[0:m, n % 4, :], ALU.add, ALU.mult).then_inc(h_ok, 1)
                        if j == HN - 1 and b:
                            add_z(b - 1)
                add_z(B - 1)

            for b in range(B):
                v.wait_ge(f_g, b + 1)
                v.tensor_tensor(fin[:, S * b:S * b + S], sT[:, S * b:S * b + S], gate[:, S * b:S * b + S], ALU.mult).then_inc(f_p, 1)
            for q in range(4):
                v.wait_ge(f_tr, q + 1)
                v.tensor_tensor(x_tok[:, 4 * q:4 * q + 4, :], bank(X, q).rearrange("p (n d) -> p n d", d=D),
                                x_tok[:, 4 * q:4 * q + 4, :], ALU.add).then_inc(f_o, 1)

        @block.gpsimd
        def _(pool):
            pool.memset(qst[64:96, :, :], 0.0).then_inc(init_p, 1)
            pool.wait_ge(init_p, 1)
            pool.memset(kst[64:96, :, :], 0.0).then_inc(init_p, 1)
            pool.wait_ge(init_p, 2)
            pool.memset(kst[96:99, :, :], 1.0).then_inc(init_p, 1)
            pool.wait_ge(init_p, 3)
            pool.memset(V32[:, :, :, DH:32], 1.0).then_inc(init_p, 1)
            pool.wait_ge(init_p, 4)
            pool.memset(latA[32:64, :], 1.0).then_inc(init_p, 1)
            pool.wait_ge(init_p, 5)
            pool.memset(xs[64:128, :, 0:1], 0.0).then_inc(init_p, 1)
            pool.wait_ge(init_p, 6)
            pool.wait_ge(init_v, 7)
            with pool.Fori(0, B) as b:
                for g in range(4):
                    pool.wait_ge(a_rec, 4 * b + g + 1)
                    pool.tensor_tensor(onorm[:, g, :], raw, rden, ALU.mult).then_inc(a_on, 1)

            def sin_part(it, t):
                pool.wait_ge(p_ev, 8 * it + 4 * t + 4)
                pool.tensor_tensor((uq, uk)[t].rearrange("p (b t) -> p b t", b=B),
                                   (qE, kE)[t].rearrange("p (b t) -> p b t", b=B),
                                   rot_sb[:, 2 * t + 1:2 * t + 2, :].broadcast_to([128, B, S]), ALU.mult).then_inc(u_ok, 1)

            def join(it, t):
                pool.wait_ge(c_ok, 2 * it + t + 1)
                pool.wait_ge(sh_ok, 2 * it + t + 1)
                pool.tensor_tensor((qr, kr)[t], (qr, kr)[t], (uq, uk)[t], ALU.add).then_inc(r_ok, 1)

            def norms(it):
                pool.wait_ge(rs, 14 * it + 14)
                stand(pool)
                pool.tensor_scalar(rk8[:], rn[:, 2:4, :], 8.0, None, ALU.mult).then_inc(po, 1)
                pool.wait_ge(po, it + 1)
                for h in range(2):
                    pool.wait_ge(rq_ok, 2 * it + h + 1)
                    pool.tensor_tensor(Mv[:, h], rk8[:, h, :].unsqueeze(2).broadcast_to([128, NW, 64]),
                                       pairs(rq_row, h), ALU.mult).then_inc(m_ok, 1)

            def normalise(it, h):
                pool.wait_ge(d_ok, 2 * it + h + 1)
                pool.tensor_tensor(Pv[:, h], Pv[:, h], pairs(dn_row, h), ALU.mult).then_inc(pn_ok, 1)

            def step(it):
                normalise(it, 0)
                normalise(it, 1)
                sin_part(it + 1, 0)
                join(it + 1, 0)
                sin_part(it + 1, 1)
                join(it + 1, 1)
                norms(it + 1)

            with pool.Fori(0, DEPTH) as L:
                for t in range(2):
                    sin_part(L * PAIRS, t)
                    join(L * PAIRS, t)
                norms(L * PAIRS)
                with pool.Fori(0, PAIRS // 2 - 1) as j:
                    for k in range(2):
                        step(L * PAIRS + j * 2 + k)
                step(L * PAIRS + PAIRS - 2)
                it = L * PAIRS + PAIRS - 1
                normalise(it, 0)
                normalise(it, 1)


def _constants():
    f = np.float32
    half = np.arange(0, HD, 2, dtype=f)
    inv = (1.0 / f(10000.0) ** (half / f(HD))).astype(f)
    t = np.arange(S, dtype=f)
    fr = (t[:, None] * inv[None, :]).astype(f)
    base = ((half + f(0.4 * HD)) / f(1.4 * HD)).astype(f)
    sc = (base[None, :] ** ((t - f(S // 2)) / f(W // 2))[:, None]).astype(f)
    cos, sin = np.cos(fr), np.sin(fr)
    e = np.arange(16)
    idx = np.concatenate([np.concatenate([16 * g + e, 16 * g + e]) for g in range(2)])
    sign = np.concatenate([np.concatenate([np.ones(16), -np.ones(16)]) for g in range(2)])
    idx, sign = np.tile(idx, 2), np.tile(sign, 2).astype(f)
    rot = []
    for s in (sc, (1.0 / sc).astype(f)):
        rot.append((cos * s)[:, idx].T)
        rot.append((sin * s)[:, idx].T * sign[:, None])
    rot = np.concatenate(rot, axis=1).astype(f)
    j, i = np.arange(W)[:, None], np.arange(W)[None, :]
    own = np.where(j <= i, 0.0, NEG)
    nxt = np.where(j >= i, 0.0, NEG)
    m = np.tile(np.concatenate([own, nxt], axis=1), (1, NW))
    m[:, -W:] = NEG
    mask = np.tile(m, (4, 1)).astype(f)
    const = np.zeros((128, 608), f)
    const[:, 0:128] = np.eye(128)
    const[:, 128:256] = np.eye(128) - 1.0 / 128
    for q in range(4):
        const[32 * q, 256:384] = 1.0
        const[32 * q + DH, 384 + 32 * q:384 + 32 * q + 32] = 1.0
    for a in range(2):
        for h in range(2):
            const[64 * h:64 * h + 64, 512 + 32 * a + 2 * a + h] = 1.0
    const[:, 576:608] = 1.0 / 128
    return rot, mask, const


def _layout(i):
    f = np.float32
    g = {k: np.asarray(v) for k, v in i.items()}
    rh = lambda a: np.ascontiguousarray(a.reshape(-1, H, DH).transpose(0, 2, 1).reshape(-1, D))
    vec = np.zeros((128, 4), f)
    vec[:, 0], vec[:, 1] = rh(g["L0_attn_bq"][None])[0], rh(g["L0_attn_bk"][None])[0]
    vec[:, 2], vec[:LAT, 3] = g["L0_attn_bo"], g["L0_attn_bl"]
    wog = np.zeros((128, 4, 128), f)
    for h in range(H):
        wog[32 * (h % 4):32 * (h % 4) + DH, h // 4] = g["L0_attn_Wo"][DH * h:DH * h + DH]
    e = np.arange(16)
    order = np.concatenate([np.concatenate([16 * q + e, 32 + 16 * q + e]) for q in range(2)])
    cols = np.concatenate([order, HD + order])
    w = g["L0_ffn_Wqkv"].reshape(DEPTH, D, 3, PAIRS, 128).transpose(0, 3, 1, 2, 4).copy()
    w[..., 0:2, :] = w[..., 0:2, :][..., cols]
    par = np.zeros((DEPTH, 128, NPAR), f)
    par[:, :, 0] = np.tile(g["L0_ffn_q_scale"][:, order], (1, 2))
    par[:, :, 1] = np.tile(g["L0_ffn_k_scale"][:, order], (1, 2))
    par[:, :, 2], par[:, :, 3], par[:, :, 4] = g["L0_ffn_ln_g"], g["L0_ffn_ln_b"], g["L0_ffn_b2"]
    for p, first in ((5, 0), (5 + HN, HID)):
        b = g["L0_ffn_b1"][:, first:first + HID]
        par[:, :, p:p + HT] = b[:, :HT * 128].reshape(DEPTH, HT, 128).transpose(0, 2, 1)
        par[:, :TAIL, p + HT] = b[:, HT * 128:]
    rot, mask, const = _constants()
    return dict(
        x=g["L0_attn_x"].reshape(T, D), wq0=rh(g["L0_attn_Wq"]), wl0=g["L0_attn_Wl"], wk0=rh(g["L0_attn_Wk"]),
        wv0=np.concatenate([g["L0_attn_Wv"], g["L0_attn_bv"][None]]), vec0=vec, wog0=wog.reshape(128, 512),
        qkv=w.reshape(DEPTH * PAIRS, D, 3, 128), wo=g["L0_ffn_Wo"].reshape(DEPTH * PAIRS, 128, D),
        par=par.transpose(1, 0, 2).reshape(128, DEPTH * NPAR), w1=g["L0_ffn_W1"], w2=g["L0_ffn_W2"],
        rot=rot, mask=mask, const=const)


def kernel(**inputs):
    import concourse.bacc as bacc
    from concourse.bass_utils import run_bass_kernel_spmd

    nc = bacc.Bacc("TRN2", target_bir_lowering=False, num_devices=1)
    arrays = {k: np.ascontiguousarray(a) for k, a in _layout(inputs).items()}
    args = {k: nc.dram_tensor(k, a.shape, mybir.dt.from_np(a.dtype), kind="ExternalInput").ap() for k, a in arrays.items()}
    out = nc.dram_tensor("out", (T, D), mybir.dt.float32, kind="ExternalOutput").ap()
    gated_stack_kernel(nc, **args, out=out)
    r = run_bass_kernel_spmd(nc, [arrays], core_ids=[0])
    return r.results[0]["out"].reshape(B, S, D)
```

```python
import concourse.bass as bass
from concourse import mybir
from contextlib import ExitStack
import numpy as np

B, S, D = 4, 512, 128
T = B * S
NT = T // 128
H = 16
DH = D // H
LAT = D // 4
DEPTH = 6
HD = 64
INNER = H * HD
PAIRS = INNER // 128
W = 32
NW = S // W
HID = int(D * 4 * 2 / 3)
HT = HID // 128
TAIL = HID - HT * 128
HN = HT + 1
NU = B * HN
NPAR = 5 + 2 * HN
NEG = -1e30


def gated_stack_kernel(nc, x, wq0, wl0, wk0, wv0, vec0, wog0, qkv, wo, par, w1, w2,
                       rot, mask, const, out):
    f32, bf16 = mybir.dt.float32, mybir.dt.bfloat16
    ALU, ACT, AX = mybir.AluOpType, mybir.ActivationFunctionType, mybir.AxisListType
    ds = bass.ds

    ctx = ExitStack()
    with ctx:
        def sb(name, shape, dt=f32):
            return ctx.enter_context(nc.sbuf_tensor(name, shape, dt))

        def sem(name):
            return ctx.enter_context(nc.semaphore(name))

        xT = sb("xT", [128, T])
        xs = sb("xs", [128, B, S])
        rot_sb = sb("rot_sb", [128, 4, S])
        mask_sb = sb("mask_sb", [128, 1024], bf16)
        const_sb = sb("const_sb", [128, 608])
        identb = sb("identb", [128, 128], bf16)
        ident = const_sb[:, 0:128]
        centre = const_sb[:, 128:256]
        pickrow = const_sb[:, 256:384]
        pickden = const_sb[:, 384:512]
        headsum = const_sb[:, 512:576].rearrange("p (a m) -> p a m", a=2)
        mean128 = const_sb[:, 576:608]
        slab = sb("slab", [128, 3, 128])
        wo_sb = sb("wo_sb", [128, 128])
        par_all = sb("par_all", [128, DEPTH * NPAR])
        par_sb = sb("par_sb", [128, NPAR])
        w1_sb = sb("w1_sb", [128, 2 * HID])
        w2_sb = sb("w2_sb", [128, HN, 128])
        big = sb("big", [128, 18 * T])

        def region(n, k=1):
            return big[:, n * T:(n + k) * T]

        qE, kE, uq, uk, xsw, qr, kr, sqq, sqk, P0, P1, oT = (region(n) for n in range(12))
        V = [region(12).rearrange("p (w c) -> p w c", c=128), region(13).rearrange("p (w c) -> p w c", c=128)]
        xsw = xsw.rearrange("p (w c) -> p w c", c=128)
        P = (P0, P1)
        Pv = [t.rearrange("p (h w c) -> p h w c", h=2, c=64) for t in P]
        PD = region(14, 4).rearrange("p (h w s b l) -> p h w s b l", h=2, s=2, b=B, l=W)
        rq_row = sb("rq_row", [128, 2, NW + 1, W])
        mx_row = sb("mx_row", [128, 2, NW + 1, W])
        dn_row = sb("dn_row", [128, 2, NW + 1, W])
        ss_t = sb("ss_t", [128, NW, 32])
        rn = sb("rn", [128, 4, NW])
        SKEW = NW + 2
        red = sb("red", [128, 2, 2 * SKEW])
        rsum = sb("rsum", [128, 2, 2 * SKEW])
        rk8 = sb("rk8", [128, 2, NW])
        mx = sb("mx", [128, 2, NW])
        dn = sb("dn", [128, 2, NW])
        rd = sb("rd", [128, 2, NW])
        xc, xsq, xn = region(0), region(1), region(2)
        gel = region(4).rearrange("p (s t) -> p s t", s=4)
        hid = region(7, 2)[:, 0:2 * HN * 512].rearrange("p (a j t) -> p a j t", a=2, j=HN)
        rstd_sb = region(10)[:, 0:512]
        x_n = region(10).rearrange("p (n d) -> p n d", d=D)
        gate, fin = region(0), region(1)
        x_in = region(16).rearrange("p (n d) -> p n d", d=D)
        s_new = region(15)
        sT, x_tok = region(12), region(13).rearrange("p (n d) -> p n d", d=D)
        mask_f = region(11)[:, 0:1024]
        qst = region(0, 2).bitcast(bf16).rearrange("p (h t) -> p h t", h=H)
        kst = region(2, 2).bitcast(bf16).rearrange("p (h t) -> p h t", h=H)
        PT = region(4, 8).rearrange("p (a c k t) -> p a c k t", a=2, c=4, k=4)
        V32 = region(12).rearrange("p (k h c) -> p k h c", k=4, c=32)
        l0 = region(13, 2)
        qf, kf, raw, rden = (l0[:, 512 * n:512 * n + 512] for n in range(4))
        onorm = region(14).rearrange("p (g t) -> p g t", g=4)
        pieces = region(17)[:, 0:1536].bitcast(bf16).rearrange("p (a c t) -> p a c t", a=2, c=3)
        latA = sb("latA", [64, 512])
        mx0 = sb("mx0", [128, H, 4])
        mneg = sb("mneg", [128, 4, H])
        mpc = sb("mpc", [128, 4, 3, H], bf16)
        mrows = sb("mrows", [48, 512], bf16)
        st6 = sb("st6", [128, NT, 6])
        mv = sb("mv", [128, NT, 2])
        rstd0, var0, var0t = sb("rstd0", [128, NT]), sb("var0", [128, NT]), sb("var0t", [128, NT])
        ssg, ssw = sb("ssg", [128, 4, NW]), sb("ssw", [128, 4 * NW])
        varw = sb("varw", [128, NT, 32])
        wl0_sb = sb("wl0_sb", [128, LAT])
        wk0_sb = sb("wk0_sb", [LAT, 128])
        wv0_sb = sb("wv0_sb", [LAT + 1, 128])
        vec0_sb = sb("vec0_sb", [128, 4])
        wog_sb = sb("wog_sb", [128, 4, 128])
        wq0_sb = sb("wq0_sb", [128, 128])
        s_dram = nc.dram_tensor("scored_out", [128, T], f32, kind="Internal").ap()
        scratch = nc.dram_tensor("piece_scratch", [2, 3, 128, 512], bf16, kind="Internal").ap()

        X = ctx.enter_context(nc.psum_tensor("X", [128, 2048], f32))
        Y = ctx.enter_context(nc.psum_tensor("Y", [128, 2048], f32))

        def pairs(t, h):
            a = t[:, h]
            return bass.AP(a.tensor, a.offset, [list(a.ap[0]), [W, NW], [1, 2 * W]])

        def bank(t, n, k=1):
            return t[:, 512 * n:512 * (n + k)]

        ld_x, ld_c, ld_w0 = [sem(f"ld_x{q}") for q in range(4)], sem("ld_c"), sem("ld_w0")
        init_v, init_p = sem("init_v"), sem("init_p")
        i_var, i_rstd, i_xn, i_tr, i_xT = (sem(n) for n in ("i_var", "i_rstd", "i_xn", "i_tr", "i_xT"))
        dv = sem("dv")
        a_q, a_lat, a_latA, a_kv, a_pc, a_v = (sem(n) for n in ("a_q", "a_lat", "a_latA", "a_kv", "a_pc", "a_v"))
        a_scr, a_st, a_s, a_mx, a_mp, a_mt, a_mr, a_mrow = (
            sem(n) for n in ("a_scr", "a_st", "a_s", "a_mx", "a_mp", "a_mt", "a_mr", "a_mrow"))
        a_sT, a_exp, a_pv, a_raw, a_den, a_rec, a_on, a_acc, a_out = (
            sem(n) for n in ("a_sT", "a_exp", "a_pv", "a_raw", "a_den", "a_rec", "a_on", "a_acc", "a_out"))
        ld_qkv, ld_wo, ld_rot, rot_ok = sem("ld_qkv"), sem("ld_wo"), sem("ld_rot"), sem("rot_ok")
        s_saved, ld_end, pd_zero, pd_ok, sq_ok = (sem(n) for n in ("s_saved", "ld_end", "pd_zero", "pd_ok", "sq_ok"))
        xs_ok, xsw_ok, par_ok = sem("xs_ok"), sem("xsw_ok"), sem("par_ok")
        p_mm, p_ev = sem("p_mm"), sem("p_ev")
        v_mm, v_ev = sem("v_mm"), sem("v_ev")
        ss_mm, ss_tr, rn_ok, rq_ok, m_ok = (sem(n) for n in ("ss_mm", "ss_tr", "rn_ok", "rq_ok", "m_ok"))
        u_ok, c_ok, sh_ok, r_ok = (sem(n) for n in ("u_ok", "c_ok", "sh_ok", "r_ok"))
        s_mm, s_rd, s_sub, e_ok, d_ok, pn_ok = (sem(n) for n in ("s_mm", "s_rd", "s_sub", "e_ok", "d_ok", "pn_ok"))
        o_mm, o_ev, y_mm, y_add = (sem(n) for n in ("o_mm", "o_ev", "y_mm", "y_add"))
        ld_w = sem("ld_w")
        c_mm, c_ev, var_mm, var_ev, rs_ok, rb_mm, t_ok, xn_ok = (
            sem(n) for n in ("c_mm", "c_ev", "var_mm", "var_ev", "rs_ok", "rb_mm", "t_ok", "xn_ok"))
        h_mm, g_ok, h_ok, z_mm, z_add = (sem(n) for n in ("h_mm", "g_ok", "h_ok", "z_mm", "z_add"))
        f_g, f_p, f_tr, f_o, st = (sem(n) for n in ("f_g", "f_p", "f_tr", "f_o", "st"))
        rs, vr = sem("rs"), sem("vr")
        sm, lo, po = sem("sm"), sem("lo"), sem("po")

        passed = sem("passed")
        block = ctx.enter_context(nc.Block())

        def stand(eng):
            eng.sem_inc(passed, 1)


        @block.sync
        def _(sp):
            xv = x.rearrange("(n p) d -> p n d", p=128)
            for q in range(4):
                sp.dma_start(x_in[:, 4 * q:4 * q + 4, :], xv[:, 4 * q:4 * q + 4, :]).then_inc(ld_x[q], 16)
            sp.dma_start(const_sb[:], const).then_inc(ld_c, 16)
            for dst, src in ((wq0_sb, wq0), (wl0_sb, wl0), (wk0_sb, wk0), (wv0_sb, wv0), (vec0_sb, vec0)):
                sp.dma_start(dst[:], src).then_inc(ld_w0, 16)
            sp.dma_start(wog_sb[:], wog0.rearrange("p (g m) -> p g m", g=4)).then_inc(ld_w0, 16)
            sp.dma_start(rot_sb[:], rot.rearrange("p (a t) -> p a t", a=4)).then_inc(ld_rot, 16)
            sp.dma_start(mask_f, mask).then_inc(ld_c, 16)
            sp.dma_start(par_all[:], par).then_inc(ld_c, 16)
            sp.dma_start(slab[:], qkv[0]).then_inc(ld_qkv, 16)
            sp.dma_start(wo_sb[:], wo[0]).then_inc(ld_wo, 16)
            sp.dma_start(w1_sb[:], w1[0]).then_inc(ld_w, 16)
            sp.dma_start(w2_sb[:, 0:HT, :], w2[0, 0:HT * 128].rearrange("(j p) n -> p j n", p=128)).then_inc(ld_w, 16)
            sp.dma_start(w2_sb[0:TAIL, HT, :], w2[0, HT * 128:HID]).then_inc(ld_w, 16)
            sp.wait_ge(init_p, 6)
            with sp.Fori(0, B) as b:
                for t in range(2):
                    sp.wait_ge(a_pc, 2 * b + 1 + t)
                    sp.dma_start(scratch[t].rearrange("c p t -> p c t"), pieces[:, t]).then_inc(a_scr, 16)
                sp.wait_ge(a_scr, 32 * b + 32)
                stand(sp)
                sp.wait_ge(a_sT, 32 * b + 1)
                for c in range(3):
                    for p in range(3):
                        sp.dma_start(qst[24 * p + 8 * c:24 * p + 8 * c + 8, :, :],
                                     scratch[0, p].rearrange("(r h) t -> r h t", h=H)).then_inc(a_st, 16)
                for c in range(3):
                    sp.dma_start(kst[24 * c:24 * c + 24, :, :],
                                 scratch[1].rearrange("c (r h) t -> (c r) h t", h=H)).then_inc(a_st, 16)
                sp.wait_ge(a_mr, b + 1)
                for p in range(3):
                    sp.dma_start(qst[96 + p:97 + p, :, :], mrows[16 * p:16 * p + 16, :]).then_inc(a_mrow, 16)

            sp.wait_ge(a_out, B + 1)
            sp.dma_start(s_dram, s_new).then_inc(s_saved, 16)

            def next_qkv(it):
                sp.wait_ge(v_mm, 4 * it + 4)
                stand(sp)
                sp.dma_start(slab[:], qkv[it + 1]).then_inc(ld_qkv, 16)

            def next_wo(it):
                sp.wait_ge(y_mm, 4 * it + 4)
                stand(sp)
                sp.dma_start(wo_sb[:], wo[it + 1]).then_inc(ld_wo, 16)

            with sp.Fori(0, DEPTH - 1) as L:
                next_qkv(L * PAIRS)
                next_qkv(L * PAIRS + 1)
                with sp.Fori(0, PAIRS - 2) as hp:
                    next_qkv(L * PAIRS + hp + 2)
                    next_wo(L * PAIRS + hp)
                sp.wait_ge(r_ok, 2 * PAIRS * L + 2 * PAIRS)
                stand(sp)
                sp.dma_start(rot_sb[:], rot.rearrange("p (a t) -> p a t", a=4)).then_inc(ld_rot, 16)
                next_wo(L * PAIRS + PAIRS - 2)
                next_wo(L * PAIRS + PAIRS - 1)
                sp.wait_ge(z_mm, 4 * L + 4)
                stand(sp)
                sp.dma_start(w1_sb[:], w1[L + 1]).then_inc(ld_w, 16)
                sp.dma_start(w2_sb[:, 0:HT, :],
                             w2[L + 1, 0:HT * 128].rearrange("(j p) n -> p j n", p=128)).then_inc(ld_w, 16)
                sp.dma_start(w2_sb[0:TAIL, HT, :], w2[L + 1, HT * 128:HID]).then_inc(ld_w, 16)
            next_qkv((DEPTH - 1) * PAIRS)
            next_qkv((DEPTH - 1) * PAIRS + 1)
            with sp.Fori(0, PAIRS - 3) as hp:
                next_qkv((DEPTH - 1) * PAIRS + hp + 2)
                next_wo((DEPTH - 1) * PAIRS + hp)
            next_wo((DEPTH - 1) * PAIRS + PAIRS - 3)
            next_wo((DEPTH - 1) * PAIRS + PAIRS - 2)
            sp.wait_ge(y_mm, 4 * DEPTH * PAIRS)
            sp.wait_ge(s_saved, 16)
            sp.dma_start(sT, s_dram).then_inc(ld_end, 16)
            sp.dma_start(x_tok, xv).then_inc(ld_end, 16)
            ov = out.rearrange("(n p) d -> p n d", p=128)
            for q in range(4):
                sp.wait_ge(f_o, q + 1)
                sp.dma_start(ov[:, 4 * q:4 * q + 4, :], x_tok[:, 4 * q:4 * q + 4, :]).then_inc(st, 16)
            sp.wait_ge(st, 64)

        @block.tensor
        def _(pe):
            def mm(o, l, r, start=True, stop=True, **k):
                return pe.matmul(o, l, r, start=start, stop=stop, **k)

            pe.wait_ge(ld_c, 48)
            pe.wait_ge(init_v, 7)
            for n in range(NT):
                pe.wait_ge(i_xn, n + 1)
                pe.transpose(Y[:, n * 128:n * 128 + 128], x_n[:, n, :], ident).then_inc(i_tr, 1)

            pe.wait_ge(ld_w0, 96)
            pe.wait_ge(i_xT, 4)
            pe.sem_inc(a_sT, 1)
            pe.sem_inc(s_mm, 2)
            pe.sem_inc(o_mm, 1)
            with pe.Fori(0, B) as b:
                xb = xT[:, ds(b * S, S)]
                pe.wait_ge(a_out, b + 1)
                mm(bank(Y, 0), wq0_sb[:], xb).then_inc(a_q, 1)
                mm(bank(Y, 1)[0:LAT], wl0_sb[:], xb).then_inc(a_lat, 1)
                pe.wait_ge(a_latA, b + 1)
                mm(bank(Y, 2), wk0_sb[:], latA[0:LAT, :])
                for k in range(4):
                    i = mm(bank(Y, 3)[:, 128 * k:128 * k + 128], latA[0:LAT + 1, 128 * k:128 * k + 128], wv0_sb[:])
                i.then_inc(a_kv, 1)
                pe.wait_ge(a_v, b + 1)
                pe.wait_ge(a_st, 192 * b + 192)
                for h in range(H):
                    if h >= 2:
                        pe.wait_ge(a_mx, 16 * b + h - 1)
                    for q in range(4):
                        i = mm(bank((X, Y)[h % 2], q), qst[0:72, h, 128 * q:128 * q + 128], kst[0:72, h, :])
                    i.then_inc(a_s, 1)
                pe.wait_ge(a_mp, b + 1)
                stand(pe)
                for q in range(4):
                    i = pe.transpose(bank(X, 0).bitcast(bf16)[0:48, 128 * q:128 * q + 128],
                                     mpc[:, q].rearrange("p c h -> p (c h)"), identb[:])
                i.then_inc(a_mt, 1)
                pe.wait_ge(a_mr, b + 1)
                pe.wait_ge(a_mrow, 48 * b + 48)
                ring = (bank(X, 0, 2), bank(X, 2, 2), bank(Y, 0, 2))

                def pv(g, k):
                    if k == 0:
                        pe.wait_ge(a_exp, 32 * b + 8 * g + 8)
                        if g:
                            pe.wait_ge(a_raw, 4 * b + g)
                    for c in range(4):
                        i = mm(bank(Y, 2)[32 * c:32 * c + 32], V32[:, k, 4 * g + c, :], PT[:, g % 2, c, k, :],
                               start=k == 0, stop=k == 3)
                    if k == 3:
                        i.then_inc(a_pv, 1)

                def den(g):
                    pe.wait_ge(a_raw, 4 * b + g + 1)
                    if g:
                        pe.wait_ge(a_rec, 4 * b + g)
                    mm(bank(Y, 3), pickden, raw).then_inc(a_den, 1)

                for h in range(H):
                    for e in range(2):
                        n = 2 * h + e
                        if n >= 3:
                            pe.wait_ge(a_exp, 32 * b + n - 2)
                        for k in range(2):
                            i = mm(ring[n % 3][:, 512 * k:512 * k + 512],
                                   kst[0:99, h, 128 * (2 * e + k):128 * (2 * e + k) + 128], qst[0:99, h, :])
                        i.then_inc(a_sT, 1)
                    if h >= 4:
                        pv(h // 4 - 1, h % 4)
                        if h % 4 == 1 and h >= 8:
                            den(h // 4 - 2)
                for k in range(4):
                    pv(3, k)
                    if k == 0:
                        den(2)
                den(3)
                for g in range(4):
                    pe.wait_ge(a_on, 4 * b + g + 1)
                    i = mm(bank(Y, 2), wog_sb[:, g, :], onorm[:, g, :], start=g == 0, stop=g == 3)
                i.then_inc(a_acc, 1)

            YB = (1, 2, 3, 0)

            def project(it, t):
                if t == 0:
                    pe.wait_ge(ld_qkv, 16 * it + 16)
                for n, b in enumerate(YB):
                    if t == 0:
                        pe.wait_ge(y_add, 4 * it + n + 1)
                    else:
                        pe.wait_ge(p_ev, 8 * it + n + 1)
                    mm(bank(Y, b), slab[:, t, :], xs[:, b, :]).then_inc(p_mm, 1)

            def project_v(it):
                for w in range(NW):
                    if w % 4 == 0:
                        pe.wait_ge(p_ev, 8 * it + 5 + (3, 0, 1, 2)[w // 4])
                    i = mm(Y[:, 128 * w:128 * w + 128], xsw[:, w, :], slab[:, 2, :])
                    if w % 4 == 3:
                        i.then_inc(v_mm, 1)

            def norms(it):
                pe.wait_ge(v_ev, 4 * it + 1)
                pe.wait_ge(sq_ok, 2 * it + 2)
                for t in range(2):
                    for b in range(B):
                        i = mm(bank(Y, 0)[32 * b:32 * b + 32], headsum[:, t, :], (sqq, sqk)[t][:, S * b:S * b + S],
                               start=t == 0, stop=t == 1)
                i.then_inc(ss_mm, 1)

            def scores(it):
                pe.wait_ge(o_ev, 4 * it + 4)
                for n in range(4):
                    mm(bank(X, n), identb[:], mask_sb[:, 512 * (n % 2):512 * (n % 2) + 512])
                pe.wait_ge(r_ok, 2 * it + 2)
                stand(pe)
                for h in range(2):
                    for w in range(NW):
                        n = 2 * W if w < NW - 1 else W
                        for b in range(B):
                            i = mm(X[32 * b:32 * b + 32, 1024 * h + 64 * w:1024 * h + 64 * w + n],
                                   kr[64 * h:64 * h + 64, S * b + W * w:S * b + W * w + W],
                                   qr[64 * h:64 * h + 64, S * b + W * w:S * b + W * w + n],
                                   start=False, stop=True, skip_group_check=True)
                    i.then_inc(s_mm, 1)

            def outputs(it, par, step):
                pe.wait_ge(s_rd, 2 * step + 2)
                pe.wait_ge(v_ev, 4 * it + 4)
                pe.wait_ge(pd_ok, 4 * it + 4)
                for w in range(NW):
                    bank_end = w % 4 == 3
                    parts = ((0, 1), (1, 2)) if bank_end else ((0, 2),)
                    for a, e in parts if w < NW - 1 else ((0, 1),):
                        c = 128 * (w + a)
                        for h in range(2):
                            i = mm(X[64 * h:64 * h + 64, c:c + 128 * (e - a)], V[par][:, w, 64 * h:64 * h + 64],
                                   PD[:, h, w, a:e].rearrange("p s b l -> p (s b l)"),
                                   start=w == 0 or a == 1, stop=w % 4 == 3 and a == 0, skip_group_check=True)
                        if bank_end and a == 0:
                            i.then_inc(o_mm, 1)

            def out_project(it, next_in_banks):
                pe.wait_ge(ld_wo, 16 * it + 16)
                for n, b in enumerate(YB):
                    pe.wait_ge(o_ev, 4 * it + n + 9)
                    pe.wait_ge(y_add, 4 * it + n + 9)
                    if next_in_banks:
                        pe.wait_ge(v_ev, 4 * it + 9 + b)
                        if b == 0:
                            pe.wait_ge(ss_tr, it + 3)
                    mm(bank(Y, b), wo_sb[:], oT[:, S * n:S * n + S]).then_inc(y_mm, 1)

            with pe.Fori(0, DEPTH) as L:
                pe.wait_ge(xs_ok, 4 * L + 2)
                project(L * PAIRS, 0)
                project(L * PAIRS, 1)
                pe.wait_ge(xsw_ok, L + 1)
                project_v(L * PAIRS)
                norms(L * PAIRS)

                def step(it, par, before):
                    if before:
                        pe.wait_ge(s_rd, 2 * it)
                    pe.wait_ge(ss_tr, it + 1)
                    pe.wait_ge(v_ev, 4 * it + 4)
                    project(it + 1, 0)
                    scores(it)
                    project(it + 1, 1)
                    if before:
                        outputs(it - 1, 1 - par, it)
                    project_v(it + 1)
                    norms(it + 1)
                    if before:
                        out_project(it - 1, True)

                step(L * PAIRS, 0, False)
                with pe.Fori(0, PAIRS // 2 - 1) as j:
                    for k in range(2):
                        step(L * PAIRS + j * 2 + k + 1, 1 - k, True)
                it = L * PAIRS + PAIRS - 1
                pe.wait_ge(s_rd, 2 * it)
                scores(it)
                outputs(it - 1, 0, it)
                out_project(it - 1, False)
                outputs(it, 1, it)
                out_project(it, False)

                pe.wait_ge(xs_ok, 4 * L + 4)
                for b in range(B):
                    mm(bank(Y, b), centre, xs[:, b, :]).then_inc(c_mm, 1)
                pe.wait_ge(o_ev, 4 * PAIRS * L + 4 * PAIRS + 8)
                for b in range(B):
                    pe.wait_ge(c_ev, 4 * L + b + 1)
                    i = mm(bank(X, 0)[32 * b:32 * b + 32], mean128, xsq[:, S * b:S * b + S])
                i.then_inc(var_mm, 1)
                pe.wait_ge(rs_ok, L + 1)
                for b in range(B):
                    mm(bank(Y, b), pickrow[32 * b:32 * b + 32, :], rstd_sb[32 * b:32 * b + 32, :]).then_inc(rb_mm, 1)
                slots = (bank(X, 0, 2), bank(X, 2, 2), bank(Y, 0, 2))
                pe.wait_ge(ld_w, 48 * L + 48)
                pe.wait_ge(t_ok, 4 * L + 4)

                def down(b):
                    if b >= 2:
                        pe.wait_ge(z_add, 4 * L + b + 3)
                    for j in range(HN):
                        pe.wait_ge(h_ok, NU * L + HN * b + j + 1)
                        k = 128 if j < HT else TAIL
                        i = mm(bank(Y, 2 + b % 2), w2_sb[0:k, j, :], hid[0:k, b % 2, j, :], start=j == 0, stop=j == HT)
                    i.then_inc(z_mm, 1)

                for b in range(B):
                    pe.wait_ge(xn_ok, 4 * L + b + 1)
                    for j in range(HN):
                        n = HN * b + j
                        if n >= 3:
                            pe.wait_ge(h_ok, NU * L + n - 2)
                        s = slots[n % 3]
                        m = 128 if j < HT else TAIL
                        mm(s[0:m, 0:512], w1_sb[:, 128 * j:128 * j + m], xn[:, S * b:S * b + S])
                        mm(s[0:m, 512:1024], w1_sb[:, HID + 128 * j:HID + 128 * j + m], xn[:, S * b:S * b + S]).then_inc(h_mm, 1)
                        if j == 1 and b:
                            down(b - 1)
                down(B - 1)

            for n in range(NT):
                pe.wait_ge(f_p, n // 4 + 1)
                i = pe.transpose(X[:, 128 * n:128 * n + 128], fin[:, 128 * n:128 * n + 128], ident)
                if n % 4 == 3:
                    i.then_inc(f_tr, 1)


        @block.scalar
        def _(act):
            def copy(o, i):
                return act.activation(o, i, ACT.Copy)

            act.sem_inc(o_ev, 8)
            act.sem_inc(a_out, 1)
            for q in range(4):
                act.wait_ge(i_tr, 4 * q + 4)
                copy(xT[:, S * q:S * q + S], bank(Y, q)).then_inc(i_xT, 1)

            act.wait_ge(ld_w0, 96)
            act.wait_ge(init_p, 6)
            with act.Fori(0, B) as b:
                act.wait_ge(a_lat, b + 1)
                act.activation(latA[0:LAT, :], bank(Y, 1)[0:LAT], ACT.Identity,
                               bias=vec0_sb[0:LAT, 3:4]).then_inc(a_latA, 1)
                ring = (bank(X, 0, 2), bank(X, 2, 2), bank(Y, 0, 2))
                for h in range(H):
                    if h % 4 == 0 and h >= 8:
                        act.wait_ge(a_pv, 4 * b + h // 4 - 1)
                    for e in range(2):
                        n = 2 * h + e
                        act.wait_ge(a_sT, 32 * b + n + 2)
                        act.activation(PT[:, (h // 4) % 2, h % 4, 2 * e:2 * e + 2, :],
                                       ring[n % 3].rearrange("p (k t) -> p k t", k=2), ACT.Exp).then_inc(a_exp, 1)
                act.wait_ge(a_acc, b + 1)
                act.activation(s_new[:, ds(b * S, S)], bank(Y, 2), ACT.Identity, bias=vec0_sb[:, 2:3]).then_inc(a_out, 1)

            def project(it, t, ns=range(4), first=False):
                if not first and ns[0] == 0:
                    act.wait_ge(u_ok, 2 * it + t - 1)
                    act.wait_ge(c_ok, 2 * it + t - 1)
                for n in ns:
                    b = (1, 2, 3, 0)[n]
                    act.wait_ge(p_mm, 8 * it + 4 * t + n + 1)
                    copy((qE, kE)[t][:, S * b:S * b + S], bank(Y, b)).then_inc(p_ev, 1)

            def squares(it):
                for t in range(2):
                    act.wait_ge(p_ev, 8 * it + 4 * t + 4)
                    act.activation((sqq, sqk)[t], (qE, kE)[t], ACT.Square).then_inc(sq_ok, 1)

            def diagonal(it, par, bs):
                act.wait_ge(pn_ok, 2 * it + 2)
                act.wait_ge(o_mm, 4 * it + 1)
                for b in bs:
                    r = slice(32 * b, 32 * b + 32)
                    copy(PD[r, :, :, :, b, :].rearrange("p h w s l -> p (h w s) l"),
                         P[par][r].rearrange("p (n l) -> p n l", l=W)).then_inc(pd_ok, 1)

            def project_v(it, par):
                for c in range(4):
                    act.wait_ge(v_mm, 4 * it + c + 1)
                    copy(V[par][:, 4 * c:4 * c + 4, :], bank(Y, c).rearrange("p (w c) -> p w c", c=128)).then_inc(v_ev, 1)

            def exps(it, par, h):
                act.wait_ge(s_sub, 2 * it + h + 1)
                Ph = P[par][:, 1024 * h:1024 * h + 1024]
                act.activation(Ph, Ph, ACT.Exp).then_inc(e_ok, 1)

            def outputs(it):
                for n in range(4):
                    act.wait_ge(o_mm, 4 * it + n + 2)
                    copy(oT[:, S * n:S * n + S], bank(X, n)).then_inc(o_ev, 1)

            def step(it, par, before):
                project(it + 1, 0)
                if before:
                    diagonal(it - 1, 1 - par, (2, 3))
                project(it + 1, 1, (0,))
                exps(it, par, 0)
                project(it + 1, 1, (1, 2, 3))
                exps(it, par, 1)
                squares(it + 1)
                if before:
                    outputs(it - 1)
                project_v(it + 1, 1 - par)
                diagonal(it, par, (0, 1))

            with act.Fori(0, DEPTH) as L:
                act.wait_ge(z_add, 4 * L + 4)
                copy(xs[0:64, :, :], xT[0:64].rearrange("p (b t) -> p b t", b=B)).then_inc(xs_ok, 1)
                act.wait_ge(par_ok, L + 1)
                project(L * PAIRS, 0, first=True)
                project(L * PAIRS, 1, first=True)
                squares(L * PAIRS)
                project_v(L * PAIRS, 0)
                step(L * PAIRS, 0, False)
                with act.Fori(0, PAIRS // 2 - 1) as j:
                    for k in range(2):
                        step(L * PAIRS + j * 2 + k + 1, 1 - k, True)
                it = L * PAIRS + PAIRS - 1
                diagonal(it - 1, 0, (2, 3))
                exps(it, 1, 0)
                exps(it, 1, 1)
                outputs(it - 1)
                diagonal(it, 1, range(B))
                outputs(it)

                act.wait_ge(y_add, 4 * PAIRS * L + 4 * PAIRS + 12)
                copy(xs[0:64, :, :], xT[0:64].rearrange("p (b t) -> p b t", b=B)).then_inc(xs_ok, 1)
                for b in range(B):
                    act.wait_ge(c_mm, 4 * L + b + 1)
                    act.activation(xsq[:, S * b:S * b + S], bank(Y, b), ACT.Square)
                    act.activation(xc[:, S * b:S * b + S], bank(Y, b), ACT.Identity,
                                   scale=par_sb[:, 2:3]).then_inc(c_ev, 1)
                for b in range(B):
                    act.wait_ge(t_ok, 4 * L + b + 1)
                    act.activation(xn[:, S * b:S * b + S], xn[:, S * b:S * b + S], ACT.Identity,
                                   bias=par_sb[:, 3:4]).then_inc(xn_ok, 1)
                slots = (bank(X, 0, 2), bank(X, 2, 2), bank(Y, 0, 2))
                for n in range(NU):
                    j = n % HN
                    act.wait_ge(h_mm, NU * L + n + 1)
                    if n >= 4:
                        act.wait_ge(h_ok, NU * L + n - 3)
                    m = 128 if j < HT else TAIL
                    act.activation(gel[0:m, n % 4, :], slots[n % 3][0:m, 512:1024], ACT.Gelu,
                                   bias=par_sb[0:m, 5 + HN + j:6 + HN + j]).then_inc(g_ok, 1)

            for b in range(B):
                if b == 0:
                    act.wait_ge(z_add, 4 * DEPTH + 4)
                act.activation(gate[:, S * b:S * b + S], xT[:, S * b:S * b + S], ACT.Silu).then_inc(f_g, 1)

        @block.vector
        def _(v):
            steps = [0]

            def link(ins, s, base):
                steps[0] += 1
                ins.then_inc(s, 1)
                v.wait_ge(s, base + steps[0])

            def bcast(a, n):
                return a.unsqueeze(2).broadcast_to([128, a.shape[1], n])

            def inverse_root(r, a, t, s, base):
                i32 = mybir.dt.int32
                link(v.tensor_scalar(r.bitcast(i32), a.bitcast(i32), -0.5, float(0x5F3759DF), ALU.mult, ALU.add), s, base)
                for _ in range(4):
                    link(v.tensor_tensor(t, r, r, ALU.mult), s, base)
                    link(v.scalar_tensor_tensor(t, t, -0.5, a, ALU.mult, ALU.mult), s, base)
                    link(v.scalar_tensor_tensor(r, t, 1.5, r, ALU.add, ALU.mult), s, base)

            v.sem_inc(y_add, 12)
            v.sem_inc(z_add, 4)
            v.wait_ge(ld_c, 48)
            v.tensor_copy(identb[:], ident).then_inc(init_v, 1)
            v.tensor_copy(mask_sb[:], mask_f).then_inc(init_v, 1)
            v.memset(red[:], NEG).then_inc(init_v, 1)
            v.memset(rsum[:], 0.0).then_inc(init_v, 1)
            v.memset(mx_row[:], 0.0).then_inc(init_v, 1)
            v.memset(dn_row[:], 1.0).then_inc(init_v, 1)
            v.memset(rq_row[:], 1.0).then_inc(init_v, 1)
            for n in range(NT):
                if n % 4 == 0:
                    v.wait_ge(ld_x[n // 4], 16)
                v.bn_stats(st6[:, n, :], x_in[:, n, :]).then_inc(i_var, 1)
            for n in range(NT):
                v.wait_ge(i_var, n + 1)
                v.bn_aggr(mv[:, n, :], st6[:, n, :]).then_inc(dv, 1)
            v.wait_ge(dv, NT)
            steps[0] = 0
            link(v.tensor_scalar(var0[:], mv[:, :, 1], 1e-5, None, ALU.add), dv, NT)
            inverse_root(rstd0[:], var0[:], var0t[:], dv, NT)
            for n in range(NT):
                v.tensor_scalar(x_n[:, n, :], x_in[:, n, :], mv[:, n, 0:1], rstd0[:, n:n + 1],
                                ALU.subtract, ALU.mult).then_inc(i_xn, 1)

            v.wait_ge(ld_w0, 96)
            with v.Fori(0, B) as b:
                steps[0] = 0
                base = 17 * b

                def split(t, src):
                    for c in range(3):
                        link(v.tensor_copy(pieces[:, t, c, :], src), lo, base)
                        if c < 2:
                            link(v.tensor_tensor(src, src, pieces[:, t, c, :], ALU.subtract), lo, base)
                v.wait_ge(a_q, b + 1)
                link(v.tensor_scalar(qf, bank(Y, 0), vec0_sb[:, 0:1], float(DH) ** -0.5, ALU.add, ALU.mult), lo, base)
                split(0, qf)
                v.sem_inc(a_pc, 1)
                v.wait_ge(a_kv, b + 1)
                link(v.tensor_scalar(kf, bank(Y, 2), vec0_sb[:, 1:2], None, ALU.add), lo, base)
                split(1, kf)
                v.sem_inc(a_pc, 1)
                v.tensor_copy(V32[:, :, :, 0:DH], bank(Y, 3).rearrange("p (k h c) -> p k h c", k=4, c=DH)).then_inc(a_v, 1)
                for h in range(H):
                    v.wait_ge(a_s, 16 * b + h + 1)
                    v.tensor_reduce(mx0[:, h, :], (X, Y)[h % 2][:, :].rearrange("p (q t) -> p q t", q=4),
                                    AX.X, ALU.max).then_inc(a_mx, 1)
                v.wait_ge(a_mx, 16 * b + 16)
                link(v.tensor_scalar(mneg[:], mx0[:].rearrange("p h q -> p q h"), -1.0, None, ALU.mult), lo, base)
                for c in range(3):
                    i = v.tensor_copy(mpc[:, :, c, :], mneg[:])
                    if c < 2:
                        link(i, lo, base)
                        link(v.tensor_tensor(mneg[:], mneg[:], mpc[:, :, c, :], ALU.subtract), lo, base)
                    else:
                        i.then_inc(a_mp, 1)
                assert steps[0] == 17, steps
                v.wait_ge(a_mt, b + 1)
                v.tensor_copy(mrows[:], bank(X, 0).bitcast(bf16)[0:48, 0:512]).then_inc(a_mr, 1)
                for g in range(4):
                    v.wait_ge(a_pv, 4 * b + g + 1)
                    if g:
                        v.wait_ge(a_on, 4 * b + g)
                    v.tensor_copy(raw, bank(Y, 2)).then_inc(a_raw, 1)
                    v.wait_ge(a_den, 4 * b + g + 1)
                    v.reciprocal(rden, bank(Y, 3)).then_inc(a_rec, 1)

            def softmax_top(it, par, h):
                Ph = P[par][:, 1024 * h:1024 * h + 1024]
                v.wait_ge(s_mm, 2 * it + h + 1 + 2)
                v.wait_ge(m_ok, 2 * it + h + 1)
                v.tensor_tensor(Ph, X[:, 1024 * h:1024 * h + 1024], Ph, ALU.mult).then_inc(s_rd, 1)
                v.wait_ge(s_rd, 2 * it + h + 1)
                base = 12 * it
                link(v.tensor_reduce(skew(red, h), Ph.rearrange("p (n c) -> p n c", c=32), AX.X, ALU.max,
                                     apply_transpose=True), sm, base)
                link(v.tensor_tensor(mx[:, h, :], red[:, h, 0:NW], red[:, h, NW + 1:2 * NW + 1], ALU.max), sm, base)
                link(v.transpose(mx_row[:, h, 0:NW, :], bcast(mx[:, h, :], 32)), sm, base)
                v.tensor_tensor(Pv[par][:, h], Pv[par][:, h], pairs(mx_row, h), ALU.subtract).then_inc(s_sub, 1)

            def softmax_sums(it, par, h):
                base = 12 * it
                v.wait_ge(e_ok, 2 * it + h + 1)
                link(v.tensor_reduce(skew(rsum, h), P[par][:, 1024 * h:1024 * h + 1024].rearrange("p (n c) -> p n c", c=32),
                                     AX.X, ALU.add, apply_transpose=True), sm, base)
                link(v.tensor_tensor(dn[:, h, :], rsum[:, h, 0:NW], rsum[:, h, NW + 1:2 * NW + 1], ALU.add), sm, base)
                link(v.reciprocal(rd[:, h, :], dn[:, h, :]), sm, base)
                v.transpose(dn_row[:, h, 0:NW, :], bcast(rd[:, h, :], 32)).then_inc(d_ok, 1)

            def skew(t, h):
                return t[:, h, :].rearrange("p (s k) -> p k s", s=2)[:, 0:NW, :]

            SWAP = [(i + 16) % 32 for i in range(32)]

            def cos_part(it, t):
                v.wait_ge(p_ev, 8 * it + 4 * t + 4)
                v.wait_ge(s_mm, 2 * it + 2)
                v.tensor_tensor((qr, kr)[t].rearrange("p (b t) -> p b t", b=B),
                                (qE, kE)[t].rearrange("p (b t) -> p b t", b=B),
                                rot_sb[:, 2 * t:2 * t + 1, :].broadcast_to([128, B, S]), ALU.mult).then_inc(c_ok, 1)

            def sin_part(it, t):
                v.wait_ge(u_ok, 2 * it + t + 1)
                stand(v)
                v.stream_shuffle((uq, uk)[t], (uq, uk)[t], SWAP).then_inc(sh_ok, 1)

            def norms_read(it):
                v.wait_ge(ss_mm, it + 1)
                v.transpose(ss_t[:].rearrange("p w c -> p (w c)"), bank(Y, 0)).then_inc(ss_tr, 1)

            def norms(it):
                v.wait_ge(ss_tr, it + 1)
                c, base, steps[0] = steps[0], 14 * it, 0
                link(v.tensor_scalar(ssg[:], ss_t[:, :, 0:4].rearrange("p w c -> p c w"), 1e-24, None, ALU.max), rs, base)
                flat = "p c w -> p (c w)"
                inverse_root(rn[:].rearrange(flat), ssg[:].rearrange(flat), ssw[:], rs, base)
                assert steps[0] == 14
                steps[0] = c
                for h in range(2):
                    v.transpose(rq_row[:, h, 0:NW, :], bcast(rn[:, h, :], 32)).then_inc(rq_ok, 1)

            xw = xT[:, :].rearrange("p (b w l) -> p w b l", b=B, l=W)

            def add_y(it):
                for n, b in enumerate((1, 2, 3, 0)):
                    v.wait_ge(y_mm, 4 * it + n + 1)
                    v.wait_ge(y_add, 4 * it + n + 9)
                    v.tensor_tensor(xw[:, 4 * n:4 * n + 4], bank(Y, b).rearrange("p (w b l) -> p w b l", w=4, b=B),
                                    xw[:, 4 * n:4 * n + 4], ALU.add).then_inc(y_add, 1)

            def step(it, par, before):
                steps[0] = 0
                softmax_top(it, par, 0)
                softmax_top(it, par, 1)
                cos_part(it + 1, 0)
                softmax_sums(it, par, 0)
                sin_part(it + 1, 0)
                softmax_sums(it, par, 1)
                cos_part(it + 1, 1)
                sin_part(it + 1, 1)
                norms_read(it + 1)
                if before:
                    add_y(it - 1)
                norms(it + 1)
                assert steps[0] == 12

            v.wait_ge(ld_c, 48)
            v.wait_ge(init_p, 6)
            v.wait_ge(i_xT, 4)
            v.wait_ge(a_out, B + 1)
            x4 = xT[:, :].rearrange("p (b t) -> p b t", b=B)
            with v.Fori(0, DEPTH) as L:
                v.wait_ge(z_add, 4 * L + 4)
                v.tensor_copy(par_sb[:], par_all[:, ds(L * NPAR, NPAR)]).then_inc(par_ok, 1)
                v.tensor_copy(xs[64:128, :, 1:S], x4[64:128, :, 0:S - 1]).then_inc(xs_ok, 1)
                v.wait_ge(par_ok, L + 1)
                v.wait_ge(ld_rot, 16 * L + 16)
                for t in range(2):
                    r = rot_sb[:, 2 * t:2 * t + 2, :]
                    v.tensor_scalar(r, r, par_sb[:, t:t + 1], None, ALU.mult).then_inc(rot_ok, 1)
                v.wait_ge(xs_ok, 4 * L + 2)
                v.tensor_copy(xsw.rearrange("p w (b l) -> p w b l", b=B),
                              xs[:].rearrange("p b (w l) -> p w b l", w=NW)).then_inc(xsw_ok, 1)
                v.wait_ge(rot_ok, 2 * L + 2)
                cos_part(L * PAIRS, 0)
                sin_part(L * PAIRS, 0)
                cos_part(L * PAIRS, 1)
                sin_part(L * PAIRS, 1)
                norms_read(L * PAIRS)
                norms(L * PAIRS)
                step(L * PAIRS, 0, False)
                with v.Fori(0, PAIRS // 2 - 1) as j:
                    for k in range(2):
                        step(L * PAIRS + j * 2 + k + 1, 1 - k, True)
                steps[0] = 0
                it = L * PAIRS + PAIRS - 1
                softmax_top(it, 1, 0)
                softmax_top(it, 1, 1)
                softmax_sums(it, 1, 0)
                softmax_sums(it, 1, 1)
                add_y(it - 1)
                add_y(it)

                v.wait_ge(y_add, 4 * PAIRS * L + 4 * PAIRS + 12)
                v.tensor_copy(xs[64:128, :, 1:S], x4[64:128, :, 0:S - 1]).then_inc(xs_ok, 1)
                v.wait_ge(var_mm, L + 1)
                steps[0] = 0
                base = 15 * L
                link(v.transpose(varw[:].rearrange("p w c -> p (w c)"), bank(X, 0)), vr, base)
                link(v.tensor_scalar(var0[:], varw[:, :, 0], 1e-5, None, ALU.add), vr, base)
                inverse_root(rstd0[:], var0[:], var0t[:], vr, base)
                v.transpose(rstd_sb.rearrange("p (w c) -> p w c", c=32), bcast(rstd0[:], 32)).then_inc(rs_ok, 1)
                assert steps[0] == 15
                for b in range(B):
                    v.wait_ge(rb_mm, 4 * L + b + 1)
                    v.tensor_tensor(xn[:, S * b:S * b + S], bank(Y, b), xc[:, S * b:S * b + S], ALU.mult).then_inc(t_ok, 1)
                slots = (bank(X, 0, 2), bank(X, 2, 2), bank(Y, 0, 2))

                def add_z(b):
                    v.wait_ge(z_mm, 4 * L + b + 1)
                    v.scalar_tensor_tensor(xT[:, S * b:S * b + S], bank(Y, 2 + b % 2), par_sb[:, 4:5],
                                           xT[:, S * b:S * b + S], ALU.add, ALU.add).then_inc(z_add, 1)

                for b in range(B):
                    for j in range(HN):
                        n = HN * b + j
                        v.wait_ge(g_ok, NU * L + n + 1)
                        if j == 0 and b >= 2:
                            v.wait_ge(z_mm, 4 * L + b - 1)
                        m = 128 if j < HT else TAIL
                        v.scalar_tensor_tensor(hid[0:m, b % 2, j, :], slots[n % 3][0:m, 0:512], par_sb[0:m, 5 + j:6 + j],
                                               gel[0:m, n % 4, :], ALU.add, ALU.mult).then_inc(h_ok, 1)
                        if j == HN - 1 and b:
                            add_z(b - 1)
                add_z(B - 1)

            v.wait_ge(ld_end, 32)
            for b in range(B):
                v.wait_ge(f_g, b + 1)
                v.tensor_tensor(fin[:, S * b:S * b + S], sT[:, S * b:S * b + S], gate[:, S * b:S * b + S], ALU.mult).then_inc(f_p, 1)
            for q in range(4):
                v.wait_ge(f_tr, q + 1)
                v.tensor_tensor(x_tok[:, 4 * q:4 * q + 4, :], bank(X, q).rearrange("p (n d) -> p n d", d=D),
                                x_tok[:, 4 * q:4 * q + 4, :], ALU.add).then_inc(f_o, 1)

        @block.gpsimd
        def _(pool):
            pool.memset(qst[64:96, :, :], 0.0).then_inc(init_p, 1)
            pool.wait_ge(init_p, 1)
            pool.memset(kst[64:96, :, :], 0.0).then_inc(init_p, 1)
            pool.wait_ge(init_p, 2)
            pool.memset(kst[96:99, :, :], 1.0).then_inc(init_p, 1)
            pool.wait_ge(init_p, 3)
            pool.memset(V32[:, :, :, DH:32], 1.0).then_inc(init_p, 1)
            pool.wait_ge(init_p, 4)
            pool.memset(latA[32:64, :], 1.0).then_inc(init_p, 1)
            pool.wait_ge(init_p, 5)
            pool.memset(xs[64:128, :, 0:1], 0.0).then_inc(init_p, 1)
            pool.wait_ge(init_p, 6)
            pool.wait_ge(init_v, 7)
            with pool.Fori(0, B) as b:
                for g in range(4):
                    pool.wait_ge(a_rec, 4 * b + g + 1)
                    pool.tensor_tensor(onorm[:, g, :], raw, rden, ALU.mult).then_inc(a_on, 1)

            def sin_part(it, t):
                pool.wait_ge(p_ev, 8 * it + 4 * t + 4)
                pool.tensor_tensor((uq, uk)[t].rearrange("p (b t) -> p b t", b=B),
                                   (qE, kE)[t].rearrange("p (b t) -> p b t", b=B),
                                   rot_sb[:, 2 * t + 1:2 * t + 2, :].broadcast_to([128, B, S]), ALU.mult).then_inc(u_ok, 1)

            def join(it, t):
                pool.wait_ge(c_ok, 2 * it + t + 1)
                pool.wait_ge(sh_ok, 2 * it + t + 1)
                pool.tensor_tensor((qr, kr)[t], (qr, kr)[t], (uq, uk)[t], ALU.add).then_inc(r_ok, 1)

            def norms(it, par):
                pool.wait_ge(rs, 14 * it + 14)
                stand(pool)
                pool.tensor_scalar(rk8[:], rn[:, 2:4, :], 8.0, None, ALU.mult).then_inc(po, 1)
                pool.wait_ge(po, it + 1)
                for h in range(2):
                    pool.wait_ge(rq_ok, 2 * it + h + 1)
                    pool.tensor_tensor(Pv[par][:, h], rk8[:, h, :].unsqueeze(2).broadcast_to([128, NW, 64]),
                                       pairs(rq_row, h), ALU.mult).then_inc(m_ok, 1)

            def normalise(it, par, h):
                pool.wait_ge(d_ok, 2 * it + h + 1)
                pool.tensor_tensor(Pv[par][:, h], Pv[par][:, h], pairs(dn_row, h), ALU.mult).then_inc(pn_ok, 1)

            def step(it, par, before):
                sin_part(it + 1, 0)
                sin_part(it + 1, 1)
                normalise(it, par, 0)
                join(it + 1, 0)
                normalise(it, par, 1)
                join(it + 1, 1)
                if before:
                    pool.wait_ge(pd_ok, 4 * it)
                norms(it + 1, 1 - par)

            pool.wait_ge(a_out, B + 1)
            pool.wait_ge(s_saved, 16)
            pool.memset(region(14, 4), 0.0).then_inc(pd_zero, 1)
            pool.wait_ge(pd_zero, 1)
            with pool.Fori(0, DEPTH) as L:
                pool.wait_ge(rot_ok, 2 * L + 2)
                sin_part(L * PAIRS, 0)
                sin_part(L * PAIRS, 1)
                join(L * PAIRS, 0)
                join(L * PAIRS, 1)
                norms(L * PAIRS, 0)
                step(L * PAIRS, 0, False)
                with pool.Fori(0, PAIRS // 2 - 1) as j:
                    for k in range(2):
                        step(L * PAIRS + j * 2 + k + 1, 1 - k, True)
                it = L * PAIRS + PAIRS - 1
                normalise(it, 1, 0)
                normalise(it, 1, 1)


def _constants():
    f = np.float32
    half = np.arange(0, HD, 2, dtype=f)
    inv = (1.0 / f(10000.0) ** (half / f(HD))).astype(f)
    t = np.arange(S, dtype=f)
    fr = (t[:, None] * inv[None, :]).astype(f)
    base = ((half + f(0.4 * HD)) / f(1.4 * HD)).astype(f)
    sc = (base[None, :] ** ((t - f(S // 2)) / f(W // 2))[:, None]).astype(f)
    cos, sin = np.cos(fr), np.sin(fr)
    e = np.arange(16)
    idx = np.concatenate([np.concatenate([16 * g + e, 16 * g + e]) for g in range(2)])
    sign = np.concatenate([np.concatenate([np.ones(16), -np.ones(16)]) for g in range(2)])
    idx, sign = np.tile(idx, 2), np.tile(sign, 2).astype(f)
    rot = []
    for s in (sc, (1.0 / sc).astype(f)):
        rot.append((cos * s)[:, idx].T)
        rot.append((sin * s)[:, idx].T * sign[:, None])
    rot = np.concatenate(rot, axis=1).astype(f)
    j, i = np.arange(W)[:, None], np.arange(W)[None, :]
    own = np.where(j <= i, 0.0, NEG)
    nxt = np.where(j >= i, 0.0, NEG)
    m = np.tile(np.concatenate([own, nxt], axis=1), (1, NW))
    m[:, -W:] = NEG
    mask = np.tile(m, (4, 1)).astype(f)
    const = np.zeros((128, 608), f)
    const[:, 0:128] = np.eye(128)
    const[:, 128:256] = np.eye(128) - 1.0 / 128
    for q in range(4):
        const[32 * q, 256:384] = 1.0
        const[32 * q + DH, 384 + 32 * q:384 + 32 * q + 32] = 1.0
    for a in range(2):
        for h in range(2):
            const[64 * h:64 * h + 64, 512 + 32 * a + 2 * a + h] = 1.0
    const[:, 576:608] = 1.0 / 128
    return rot, mask, const


def _layout(i):
    f = np.float32
    g = {k: np.asarray(v) for k, v in i.items()}
    rh = lambda a: np.ascontiguousarray(a.reshape(-1, H, DH).transpose(0, 2, 1).reshape(-1, D))
    vec = np.zeros((128, 4), f)
    vec[:, 0], vec[:, 1] = rh(g["L0_attn_bq"][None])[0], rh(g["L0_attn_bk"][None])[0]
    vec[:, 2], vec[:LAT, 3] = g["L0_attn_bo"], g["L0_attn_bl"]
    wog = np.zeros((128, 4, 128), f)
    for h in range(H):
        wog[32 * (h % 4):32 * (h % 4) + DH, h // 4] = g["L0_attn_Wo"][DH * h:DH * h + DH]
    e = np.arange(16)
    order = np.concatenate([np.concatenate([16 * q + e, 32 + 16 * q + e]) for q in range(2)])
    cols = np.concatenate([order, HD + order])
    w = g["L0_ffn_Wqkv"].reshape(DEPTH, D, 3, PAIRS, 128).transpose(0, 3, 1, 2, 4).copy()
    w[..., 0:2, :] = w[..., 0:2, :][..., cols]
    par = np.zeros((DEPTH, 128, NPAR), f)
    par[:, :, 0] = np.tile(g["L0_ffn_q_scale"][:, order], (1, 2))
    par[:, :, 1] = np.tile(g["L0_ffn_k_scale"][:, order], (1, 2))
    par[:, :, 2], par[:, :, 3], par[:, :, 4] = g["L0_ffn_ln_g"], g["L0_ffn_ln_b"], g["L0_ffn_b2"]
    for p, first in ((5, 0), (5 + HN, HID)):
        b = g["L0_ffn_b1"][:, first:first + HID]
        par[:, :, p:p + HT] = b[:, :HT * 128].reshape(DEPTH, HT, 128).transpose(0, 2, 1)
        par[:, :TAIL, p + HT] = b[:, HT * 128:]
    rot, mask, const = _constants()
    return dict(
        x=g["L0_attn_x"].reshape(T, D), wq0=rh(g["L0_attn_Wq"]), wl0=g["L0_attn_Wl"], wk0=rh(g["L0_attn_Wk"]),
        wv0=np.concatenate([g["L0_attn_Wv"], g["L0_attn_bv"][None]]), vec0=vec, wog0=wog.reshape(128, 512),
        qkv=w.reshape(DEPTH * PAIRS, D, 3, 128), wo=g["L0_ffn_Wo"].reshape(DEPTH * PAIRS, 128, D),
        par=par.transpose(1, 0, 2).reshape(128, DEPTH * NPAR), w1=g["L0_ffn_W1"], w2=g["L0_ffn_W2"],
        rot=rot, mask=mask, const=const)


def kernel(**inputs):
    import concourse.bacc as bacc
    from concourse.bass_utils import run_bass_kernel_spmd

    nc = bacc.Bacc("TRN2", target_bir_lowering=False, num_devices=1)
    arrays = {k: np.ascontiguousarray(a) for k, a in _layout(inputs).items()}
    args = {k: nc.dram_tensor(k, a.shape, mybir.dt.from_np(a.dtype), kind="ExternalInput").ap() for k, a in arrays.items()}
    out = nc.dram_tensor("out", (T, D), mybir.dt.float32, kind="ExternalOutput").ap()
    gated_stack_kernel(nc, **args, out=out)
    r = run_bass_kernel_spmd(nc, [arrays], core_ids=[0])
    return r.results[0]["out"].reshape(B, S, D)
```

```python
import concourse.bass as bass
from concourse import mybir
from contextlib import ExitStack
import numpy as np

B, S, D = 4, 512, 128
T = B * S
NT = T // 128
H = 16
DH = D // H
LAT = D // 4
DEPTH = 6
HD = 64
INNER = H * HD
PAIRS = INNER // 128
W = 32
NW = S // W
HID = int(D * 4 * 2 / 3)
HT = HID // 128
TAIL = HID - HT * 128
HN = HT + 1
NU = B * HN
NPAR = 5 + 2 * HN
NEG = -1e30


def gated_stack_kernel(nc, x, wq0, wl0, wk0, wv0, vec0, wog0, qkv, wo, par, w1, w2,
                       rot, mask, const, out):
    f32, bf16 = mybir.dt.float32, mybir.dt.bfloat16
    ALU, ACT, AX = mybir.AluOpType, mybir.ActivationFunctionType, mybir.AxisListType
    ds = bass.ds

    ctx = ExitStack()
    with ctx:
        def sb(name, shape, dt=f32):
            return ctx.enter_context(nc.sbuf_tensor(name, shape, dt))

        def sem(name):
            return ctx.enter_context(nc.semaphore(name))

        xT = sb("xT", [128, T])
        xs = sb("xs", [128, B, S])
        rot_sb = sb("rot_sb", [128, 4, S])
        mask_sb = sb("mask_sb", [128, 1024], bf16)
        const_sb = sb("const_sb", [128, 608])
        identb = sb("identb", [128, 128], bf16)
        ident = const_sb[:, 0:128]
        centre = const_sb[:, 128:256]
        pickrow = const_sb[:, 256:384]
        pickden = const_sb[:, 384:512]
        headsum = const_sb[:, 512:576].rearrange("p (a m) -> p a m", a=2)
        mean128 = const_sb[:, 576:608]
        slab = sb("slab", [128, 3, 128])
        wo_sb = sb("wo_sb", [128, 128])
        par_all = sb("par_all", [128, DEPTH * NPAR])
        par_sb = sb("par_sb", [128, NPAR])
        w1_sb = sb("w1_sb", [128, 2 * HID])
        w2_sb = sb("w2_sb", [128, HN, 128])
        big = sb("big", [128, 18 * T])

        def region(n, k=1):
            return big[:, n * T:(n + k) * T]

        qE, kE, uq, uk, xsw, qr, kr, sqq, sqk, P0, P1, oT = (region(n) for n in range(12))
        V = [region(12).rearrange("p (w c) -> p w c", c=128), region(13).rearrange("p (w c) -> p w c", c=128)]
        xsw = xsw.rearrange("p (w c) -> p w c", c=128)
        P = (P0, P1)
        Pv = [t.rearrange("p (h w c) -> p h w c", h=2, c=64) for t in P]
        PD = region(14, 4).rearrange("p (h w s b l) -> p h w s b l", h=2, s=2, b=B, l=W)
        rq_row = sb("rq_row", [128, 2, NW + 1, W])
        mx_row = sb("mx_row", [128, 2, NW + 1, W])
        dn_row = sb("dn_row", [128, 2, NW + 1, W])
        ss_t = sb("ss_t", [128, NW, 32])
        rn = sb("rn", [128, 4, NW])
        SKEW = NW + 2
        red = sb("red", [128, 2, 2 * SKEW])
        rsum = sb("rsum", [128, 2, 2 * SKEW])
        rk8 = sb("rk8", [128, 2, NW])
        mx = sb("mx", [128, 2, NW])
        dn = sb("dn", [128, 2, NW])
        rd = sb("rd", [128, 2, NW])
        xc, xsq, xn = region(0), region(1), region(2)
        gel = region(4).rearrange("p (s t) -> p s t", s=4)
        hid = region(7, 2)[:, 0:2 * HN * 512].rearrange("p (a j t) -> p a j t", a=2, j=HN)
        rstd_sb = region(10)[:, 0:512]
        x_n = region(10).rearrange("p (n d) -> p n d", d=D)
        gate, fin = region(0), region(1)
        x_in = region(17).rearrange("p (n d) -> p n d", d=D)
        s_new = region(17)
        sT, x_tok = region(12), region(13).rearrange("p (n d) -> p n d", d=D)
        mask_f = region(11)[:, 0:1024]
        qst = [region(n, 2).bitcast(bf16).rearrange("p (h t) -> p h t", h=H) for n in (0, 4)]
        kst = [region(n, 2).bitcast(bf16).rearrange("p (h t) -> p h t", h=H) for n in (2, 6)]
        PT = [region(n, 2).rearrange("p (c k t) -> p c k t", c=4, k=2) for n in (8, 10, 12)]
        V32 = region(14).rearrange("p (k h c) -> p k h c", k=4, c=32)
        l0 = region(15)
        qf, kf, raw, rden = (l0[:, 512 * n:512 * n + 512] for n in range(4))
        onorm = region(16).rearrange("p (g t) -> p g t", g=4)
        pieces = rot_sb[:].rearrange("p a t -> p (a t)")[:, 0:1536].bitcast(bf16).rearrange("p (a c t) -> p a c t", a=2, c=3)
        latA = sb("latA", [64, 512])
        mx0 = sb("mx0", [128, H, 4])
        mneg = sb("mneg", [128, 4, H])
        mpc = sb("mpc", [128, 4, 3, H], bf16)
        mrows = sb("mrows", [48, 512], bf16)
        st6 = sb("st6", [128, NT, 6])
        mv = sb("mv", [128, NT, 2])
        rstd0, var0, var0t = sb("rstd0", [128, NT]), sb("var0", [128, NT]), sb("var0t", [128, NT])
        ssg, ssw = sb("ssg", [128, 4, NW]), sb("ssw", [128, 4 * NW])
        varw = sb("varw", [128, NT, 32])
        rawT, rq0 = varw, var0
        wl0_sb = sb("wl0_sb", [128, LAT])
        wk0_sb = sb("wk0_sb", [LAT, 128])
        wv0_sb = sb("wv0_sb", [LAT + 1, 128])
        vec0_sb = sb("vec0_sb", [128, 4])
        wog_sb = sb("wog_sb", [128, 4, 128])
        wq0_sb = sb("wq0_sb", [128, 128])
        s_dram = nc.dram_tensor("scored_out", [128, T], f32, kind="Internal").ap()
        scratch = nc.dram_tensor("piece_scratch", [2, 3, 128, 512], bf16, kind="Internal").ap()

        X = ctx.enter_context(nc.psum_tensor("X", [128, 2048], f32))
        Y = ctx.enter_context(nc.psum_tensor("Y", [128, 2048], f32))

        def pairs(t, h):
            a = t[:, h]
            return bass.AP(a.tensor, a.offset, [list(a.ap[0]), [W, NW], [1, 2 * W]])

        def bank(t, n, k=1):
            return t[:, 512 * n:512 * (n + k)]

        ld_x, ld_c, ld_w0 = [sem(f"ld_x{q}") for q in range(4)], sem("ld_c"), sem("ld_w0")
        init_v, init_p = sem("init_v"), sem("init_p")
        i_var, i_rstd, i_xn, i_tr, i_xT = (sem(n) for n in ("i_var", "i_rstd", "i_xn", "i_tr", "i_xT"))
        dv = sem("dv")
        a_q, a_lat, a_latA, a_k, a_vmm, a_pc, a_v, a_qf, a_kf = (
            sem(n) for n in ("a_q", "a_lat", "a_latA", "a_k", "a_vmm", "a_pc", "a_v", "a_qf", "a_kf"))
        a_scr, a_st, a_s, a_mx, a_mp, a_mt, a_mr, a_mrow = (
            sem(n) for n in ("a_scr", "a_st", "a_s", "a_mx", "a_mp", "a_mt", "a_mr", "a_mrow"))
        a_rT = sem("a_rT")
        a_sT, a_exp, a_pv, a_raw, a_den, a_rec, a_on, a_acc, a_out = (
            sem(n) for n in ("a_sT", "a_exp", "a_pv", "a_raw", "a_den", "a_rec", "a_on", "a_acc", "a_out"))
        ld_qkv, ld_wo, ld_rot, rot_ok = sem("ld_qkv"), sem("ld_wo"), sem("ld_rot"), sem("rot_ok")
        s_saved, ld_end, pd_zero, pd_ok, sq_ok, xs_zero = (sem(n) for n in ("s_saved", "ld_end", "pd_zero", "pd_ok", "sq_ok", "xs_zero"))
        xs_ok, xsw_ok, par_ok = sem("xs_ok"), sem("xsw_ok"), sem("par_ok")
        p_mm, p_ev = sem("p_mm"), sem("p_ev")
        v_mm, v_ev = sem("v_mm"), sem("v_ev")
        ss_mm, ss_tr, rn_ok, rq_ok, m_ok = (sem(n) for n in ("ss_mm", "ss_tr", "rn_ok", "rq_ok", "m_ok"))
        u_ok, c_ok, sh_ok, r_ok = (sem(n) for n in ("u_ok", "c_ok", "sh_ok", "r_ok"))
        s_mm, s_rd, s_sub, e_ok, d_ok, pn_ok = (sem(n) for n in ("s_mm", "s_rd", "s_sub", "e_ok", "d_ok", "pn_ok"))
        o_mm, o_ev, y_mm, y_add = (sem(n) for n in ("o_mm", "o_ev", "y_mm", "y_add"))
        ld_w = sem("ld_w")
        c_mm, c_ev, var_mm, var_ev, rs_ok, rb_mm, t_ok, xn_ok = (
            sem(n) for n in ("c_mm", "c_ev", "var_mm", "var_ev", "rs_ok", "rb_mm", "t_ok", "xn_ok"))
        h_mm, g_ok, h_ok, z_mm, z_add = (sem(n) for n in ("h_mm", "g_ok", "h_ok", "z_mm", "z_add"))
        f_g, f_p, f_tr, f_o, st = (sem(n) for n in ("f_g", "f_p", "f_tr", "f_o", "st"))
        rs, vr = sem("rs"), sem("vr")
        sm, lo, po = sem("sm"), sem("lo"), sem("po")

        passed = sem("passed")
        block = ctx.enter_context(nc.Block())

        BESIDE = 20
        AHEAD = 32 - BESIDE
        top_slots = (bank(X, 0, 2), bank(X, 2, 2), bank(Y, 0, 2))

        def stand(eng):
            eng.sem_inc(passed, 1)


        @block.sync
        def _(sp):
            xv = x.rearrange("(n p) d -> p n d", p=128)
            for q in range(4):
                sp.dma_start(x_in[:, 4 * q:4 * q + 4, :], xv[:, 4 * q:4 * q + 4, :]).then_inc(ld_x[q], 16)
            sp.dma_start(const_sb[:], const).then_inc(ld_c, 16)
            for dst, src in ((wq0_sb, wq0), (wl0_sb, wl0), (wk0_sb, wk0), (wv0_sb, wv0), (vec0_sb, vec0)):
                sp.dma_start(dst[:], src).then_inc(ld_w0, 16)
            sp.dma_start(wog_sb[:], wog0.rearrange("p (g m) -> p g m", g=4)).then_inc(ld_w0, 16)
            sp.dma_start(mask_f, mask).then_inc(ld_c, 16)
            sp.dma_start(par_all[:], par).then_inc(ld_c, 16)
            sp.dma_start(slab[:], qkv[0]).then_inc(ld_qkv, 16)
            sp.dma_start(wo_sb[:], wo[0]).then_inc(ld_wo, 16)
            sp.dma_start(w1_sb[:], w1[0]).then_inc(ld_w, 16)
            sp.dma_start(w2_sb[:, 0:HT, :], w2[0, 0:HT * 128].rearrange("(j p) n -> p j n", p=128)).then_inc(ld_w, 16)
            sp.dma_start(w2_sb[0:TAIL, HT, :], w2[0, HT * 128:HID]).then_inc(ld_w, 16)
            sp.wait_ge(init_p, 9)

            def stacks(b, par):
                for t in range(2):
                    sp.wait_ge(a_pc, 2 * b + 1 + t)
                    sp.dma_start(scratch[t].rearrange("c p t -> p c t"), pieces[:, t]).then_inc(a_scr, 16)
                sp.wait_ge(a_scr, 32 * b + 32)
                stand(sp)
                sp.wait_ge(a_sT, 32 * b + 32)
                for c in range(3):
                    for p in range(3):
                        sp.dma_start(qst[par][24 * p + 8 * c:24 * p + 8 * c + 8, :, :],
                                     scratch[0, p].rearrange("(r h) t -> r h t", h=H)).then_inc(a_st, 16)
                for c in range(3):
                    sp.dma_start(kst[par][24 * c:24 * c + 24, :, :],
                                 scratch[1].rearrange("c (r h) t -> (c r) h t", h=H)).then_inc(a_st, 16)
                sp.wait_ge(a_mr, b + 1)
                for p in range(3):
                    sp.dma_start(qst[par][96 + p:97 + p, :, :], mrows[16 * p:16 * p + 16, :]).then_inc(a_mrow, 16)

            with sp.Fori(0, B // 2) as j:
                for k in range(2):
                    stacks(2 * j + k, k)
            sp.dma_start(rot_sb[:], rot.rearrange("p (a t) -> p a t", a=4)).then_inc(ld_rot, 16)
            sp.wait_ge(a_out, B + 1)
            sp.dma_start(s_dram, s_new).then_inc(s_saved, 16)

            def next_qkv(it):
                sp.wait_ge(v_mm, 4 * it + 4)
                stand(sp)
                sp.dma_start(slab[:], qkv[it + 1]).then_inc(ld_qkv, 16)

            def next_wo(it):
                sp.wait_ge(y_mm, 4 * it + 4)
                stand(sp)
                sp.dma_start(wo_sb[:], wo[it + 1]).then_inc(ld_wo, 16)

            with sp.Fori(0, DEPTH - 1) as L:
                next_qkv(L * PAIRS)
                next_qkv(L * PAIRS + 1)
                with sp.Fori(0, PAIRS - 2) as hp:
                    next_qkv(L * PAIRS + hp + 2)
                    next_wo(L * PAIRS + hp)
                sp.wait_ge(r_ok, 2 * PAIRS * L + 2 * PAIRS)
                stand(sp)
                sp.dma_start(rot_sb[:], rot.rearrange("p (a t) -> p a t", a=4)).then_inc(ld_rot, 16)
                next_wo(L * PAIRS + PAIRS - 2)
                next_wo(L * PAIRS + PAIRS - 1)
                sp.wait_ge(z_mm, 4 * L + 4)
                stand(sp)
                sp.dma_start(w1_sb[:], w1[L + 1]).then_inc(ld_w, 16)
                sp.dma_start(w2_sb[:, 0:HT, :],
                             w2[L + 1, 0:HT * 128].rearrange("(j p) n -> p j n", p=128)).then_inc(ld_w, 16)
                sp.dma_start(w2_sb[0:TAIL, HT, :], w2[L + 1, HT * 128:HID]).then_inc(ld_w, 16)
            next_qkv((DEPTH - 1) * PAIRS)
            next_qkv((DEPTH - 1) * PAIRS + 1)
            with sp.Fori(0, PAIRS - 3) as hp:
                next_qkv((DEPTH - 1) * PAIRS + hp + 2)
                next_wo((DEPTH - 1) * PAIRS + hp)
            next_wo((DEPTH - 1) * PAIRS + PAIRS - 3)
            next_wo((DEPTH - 1) * PAIRS + PAIRS - 2)
            sp.wait_ge(y_mm, 4 * DEPTH * PAIRS)
            sp.wait_ge(s_saved, 16)
            sp.dma_start(sT, s_dram).then_inc(ld_end, 16)
            sp.dma_start(x_tok, xv).then_inc(ld_end, 16)
            ov = out.rearrange("(n p) d -> p n d", p=128)
            for q in range(4):
                sp.wait_ge(f_o, q + 1)
                sp.dma_start(ov[:, 4 * q:4 * q + 4, :], x_tok[:, 4 * q:4 * q + 4, :]).then_inc(st, 16)
            sp.wait_ge(st, 64)

        @block.tensor
        def _(pe):
            def mm(o, l, r, start=True, stop=True, **k):
                return pe.matmul(o, l, r, start=start, stop=stop, **k)

            pe.wait_ge(ld_c, 48)
            pe.wait_ge(init_v, 7)
            for n in range(NT):
                pe.wait_ge(i_xn, n + 1)
                pe.transpose(Y[:, n * 128:n * 128 + 128], x_n[:, n, :], ident).then_inc(i_tr, 1)

            pe.wait_ge(ld_w0, 96)
            pe.wait_ge(i_xT, 4)
            pe.sem_inc(a_sT, 64)
            pe.sem_inc(s_mm, 2)
            pe.sem_inc(o_mm, 1)

            def l0_qk(b):
                xb = xT[:, ds(b * S, S)]
                mm(bank(Y, 0), wq0_sb[:], xb).then_inc(a_q, 1)
                mm(bank(Y, 1)[0:LAT], wl0_sb[:], xb).then_inc(a_lat, 1)
                pe.wait_ge(a_latA, b + 1)
                pe.wait_ge(a_qf, b + 1)
                mm(bank(Y, 0), wk0_sb[:], latA[0:LAT, :]).then_inc(a_k, 1)

            def l0_v(b):
                for k in range(4):
                    i = mm(bank(Y, 2)[:, 128 * k:128 * k + 128], latA[0:LAT + 1, 128 * k:128 * k + 128], wv0_sb[:])
                i.then_inc(a_vmm, 1)

            def l0_top(b, par, n):
                h, q = n // 4, n % 4
                if n == 0:
                    pe.wait_ge(a_kf, b + 1)
                    pe.wait_ge(a_st, 192 * b + 192)
                if n >= 2:
                    pe.wait_ge(a_mx, 64 * b + n - 1)
                mm(bank(Y, n % 2), qst[par][0:72, h, 128 * q:128 * q + 128], kst[par][0:72, h, :]).then_inc(a_s, 1)

            def l0_top2(b, par, m, first):
                if m == 0:
                    pe.wait_ge(a_kf, b + 1)
                    pe.wait_ge(a_st, 192 * b + 192)
                if m >= 3:
                    pe.wait_ge(a_mx, 64 * b + 2 * m - 4)
                for n in (2 * m, 2 * m + 1):
                    h, q = n // 4, n % 4
                    mm(top_slots[(m - first) % 3][:, 512 * (n % 2):512 * (n % 2) + 512],
                       qst[par][0:72, h, 128 * q:128 * q + 128], kst[par][0:72, h, :]).then_inc(a_s, 1)

            def l0_rows(b):
                pe.wait_ge(a_mp, b + 1)
                stand(pe)
                for q in range(4):
                    i = pe.transpose(bank(Y, 0).bitcast(bf16)[0:48, 128 * q:128 * q + 128],
                                     mpc[:, q].rearrange("p c h -> p (c h)"), identb[:])
                i.then_inc(a_mt, 1)
                pe.wait_ge(a_mr, b + 1)

            def l0_pv(b, lot, k):
                g = lot // 2
                if k == 0:
                    pe.wait_ge(a_exp, 32 * b + 4 * lot + 4)
                    if lot == 0:
                        pe.wait_ge(a_v, b + 1)
                    elif lot % 2 == 0:
                        pe.wait_ge(a_raw, 4 * b + g)
                first, last = lot % 2 == 0 and k == 0, lot % 2 == 1 and k == 1
                for c in range(4):
                    i = mm(bank(Y, 2)[32 * c:32 * c + 32], V32[:, 2 * (lot % 2) + k, 4 * g + c, :],
                           PT[lot % 3][:, c, k, :], start=first, stop=last)
                if k == 1:
                    i.then_inc(a_pv, 1)

            def l0_unit(b, par, lot, c):
                if lot == 0 and c == 0:
                    pe.wait_ge(a_mrow, 48 * b + 48)
                h, n = 4 * (lot // 2) + c, 4 * lot + c
                if n >= 2:
                    pe.wait_ge(a_exp, 32 * b + n - 1)
                for k in range(2):
                    t = 2 * (lot % 2) + k
                    i = mm(bank(X, 2 * (n % 2) + k), kst[par][0:99, h, 128 * t:128 * t + 128], qst[par][0:99, h, :])
                i.then_inc(a_sT, 1)
                if c % 2 and lot:
                    l0_pv(b, lot - 1, c // 2)

            def l0_out(b, g):
                pe.wait_ge(a_on, 4 * b + g + 1)
                if g == 0:
                    pe.wait_ge(a_out, b + 1)
                i = mm(bank(Y, 3), wog_sb[:, g, :], onorm[:, g, :], start=g == 0, stop=g == 3)
                if g == 3:
                    i.then_inc(a_acc, 1)

            def l0_step(b, par):
                l0_qk(b + 1)
                for u in range(32):
                    l0_unit(b, par, u // 4, u % 4)
                    if u >= BESIDE:
                        l0_top(b + 1, 1 - par, u - BESIDE)
                l0_pv(b, 7, 0)
                l0_pv(b, 7, 1)
                for m in range(AHEAD // 2, 32):
                    l0_top2(b + 1, 1 - par, m, AHEAD // 2)
                    if m % 2 and 10 < m < 19:
                        l0_out(b, (m - 11) // 2)
                    if m == 21:
                        l0_v(b + 1)
                l0_rows(b + 1)

            l0_qk(0)
            l0_v(0)
            for m in range(32):
                l0_top2(0, 0, m, 0)
            l0_rows(0)
            with pe.Fori(0, B // 2 - 1) as j:
                for k in range(2):
                    l0_step(2 * j + k, k)
            l0_step(B - 2, 0)
            for u in range(32):
                l0_unit(B - 1, 1, u // 4, u % 4)
            l0_pv(B - 1, 7, 0)
            l0_pv(B - 1, 7, 1)
            for g in range(4):
                l0_out(B - 1, g)

            YB = (1, 2, 3, 0)

            def project(it, t, ns=range(4)):
                if t == 0:
                    pe.wait_ge(ld_qkv, 16 * it + 16)
                for n in ns:
                    b = YB[n]
                    if t == 0:
                        pe.wait_ge(y_add, 4 * it + n + 1)
                    else:
                        pe.wait_ge(p_ev, 8 * it + n + 1)
                    mm(bank(Y, b), slab[:, t, :], xs[:, b, :]).then_inc(p_mm, 1)

            def project_v(it):
                for w in range(NW):
                    if w % 4 == 0:
                        pe.wait_ge(p_ev, 8 * it + 5 + (3, 0, 1, 2)[w // 4])
                    i = mm(Y[:, 128 * w:128 * w + 128], xsw[:, w, :], slab[:, 2, :])
                    if w % 4 == 3:
                        i.then_inc(v_mm, 1)

            def norms(it):
                pe.wait_ge(v_ev, 4 * it + 1)
                pe.wait_ge(sq_ok, 2 * it + 2)
                for t in range(2):
                    for b in range(B):
                        i = mm(bank(Y, 0)[32 * b:32 * b + 32], headsum[:, t, :], (sqq, sqk)[t][:, S * b:S * b + S],
                               start=t == 0, stop=t == 1)
                i.then_inc(ss_mm, 1)

            BESIDE_S = {(0, 7): (0, 3)}

            def scores(it, beside=False):
                pe.wait_ge(o_ev, 4 * it + 4)
                for n in range(4):
                    mm(bank(X, n), identb[:], mask_sb[:, 512 * (n % 2):512 * (n % 2) + 512])
                pe.wait_ge(r_ok, 2 * it + 2)
                stand(pe)
                for h in range(2):
                    for w in range(NW):
                        n = 2 * W if w < NW - 1 else W
                        for b in range(B):
                            i = mm(X[32 * b:32 * b + 32, 1024 * h + 64 * w:1024 * h + 64 * w + n],
                                   kr[64 * h:64 * h + 64, S * b + W * w:S * b + W * w + W],
                                   qr[64 * h:64 * h + 64, S * b + W * w:S * b + W * w + n],
                                   start=False, stop=True, skip_group_check=True)
                        if beside and (h, w) in BESIDE_S:
                            t, n = BESIDE_S[h, w]
                            project(it + 1, t, (n,))
                    i.then_inc(s_mm, 1)

            def outputs(it, par, step):
                pe.wait_ge(s_rd, 2 * step + 2)
                pe.wait_ge(v_ev, 4 * it + 4)
                pe.wait_ge(pd_ok, 4 * it + 4)
                for w in range(NW):
                    bank_end = w % 4 == 3
                    parts = ((0, 1), (1, 2)) if bank_end else ((0, 2),)
                    for a, e in parts if w < NW - 1 else ((0, 1),):
                        c = 128 * (w + a)
                        for h in range(2):
                            i = mm(X[64 * h:64 * h + 64, c:c + 128 * (e - a)], V[par][:, w, 64 * h:64 * h + 64],
                                   PD[:, h, w, a:e].rearrange("p s b l -> p (s b l)"),
                                   start=w == 0 or a == 1, stop=w % 4 == 3 and a == 0, skip_group_check=True)
                        if bank_end and a == 0:
                            i.then_inc(o_mm, 1)

            def out_project(it, next_in_banks):
                pe.wait_ge(ld_wo, 16 * it + 16)
                for n, b in enumerate(YB):
                    pe.wait_ge(o_ev, 4 * it + n + 9)
                    pe.wait_ge(y_add, 4 * it + n + 9)
                    if next_in_banks:
                        pe.wait_ge(v_ev, 4 * it + 9 + b)
                        if b == 0:
                            pe.wait_ge(ss_tr, it + 3)
                    mm(bank(Y, b), wo_sb[:], oT[:, S * n:S * n + S]).then_inc(y_mm, 1)

            with pe.Fori(0, DEPTH) as L:
                pe.wait_ge(xs_ok, 4 * L + 2)
                project(L * PAIRS, 0)
                project(L * PAIRS, 1)
                pe.wait_ge(xsw_ok, L + 1)
                project_v(L * PAIRS)
                norms(L * PAIRS)

                def start(it):
                    pe.wait_ge(ss_tr, it + 1)
                    pe.wait_ge(v_ev, 4 * it + 4)

                def step(it, par):
                    pe.wait_ge(s_rd, 2 * it)
                    start(it)
                    project(it + 1, 0, range(3))
                    scores(it, True)
                    project(it + 1, 1, range(0, 4))
                    outputs(it - 1, 1 - par, it)
                    project_v(it + 1)
                    norms(it + 1)
                    out_project(it - 1, True)

                it = L * PAIRS
                start(it)
                project(it + 1, 0)
                project(it + 1, 1)
                scores(it)
                project_v(it + 1)
                norms(it + 1)
                with pe.Fori(0, PAIRS // 2 - 1) as j:
                    for k in range(2):
                        step(L * PAIRS + j * 2 + k + 1, 1 - k)
                it = L * PAIRS + PAIRS - 1
                pe.wait_ge(s_rd, 2 * it)
                scores(it)
                outputs(it - 1, 0, it)
                out_project(it - 1, False)
                outputs(it, 1, it)
                out_project(it, False)

                pe.wait_ge(xs_ok, 4 * L + 4)
                for b in range(B):
                    mm(bank(Y, b), centre, xs[:, b, :]).then_inc(c_mm, 1)
                pe.wait_ge(o_ev, 4 * PAIRS * L + 4 * PAIRS + 8)
                for b in range(B):
                    pe.wait_ge(c_ev, 4 * L + b + 1)
                    i = mm(bank(X, 0)[32 * b:32 * b + 32], mean128, xsq[:, S * b:S * b + S])
                i.then_inc(var_mm, 1)
                pe.wait_ge(rs_ok, L + 1)
                for b in range(B):
                    mm(bank(Y, b), pickrow[32 * b:32 * b + 32, :], rstd_sb[32 * b:32 * b + 32, :]).then_inc(rb_mm, 1)
                slots = (bank(X, 0, 2), bank(X, 2, 2), bank(Y, 0, 2))
                pe.wait_ge(ld_w, 48 * L + 48)
                pe.wait_ge(t_ok, 4 * L + 4)

                def down(b):
                    if b >= 2:
                        pe.wait_ge(z_add, 4 * L + b + 3)
                    for j in range(HN):
                        pe.wait_ge(h_ok, NU * L + HN * b + j + 1)
                        k = 128 if j < HT else TAIL
                        i = mm(bank(Y, 2 + b % 2), w2_sb[0:k, j, :], hid[0:k, b % 2, j, :], start=j == 0, stop=j == HT)
                    i.then_inc(z_mm, 1)

                for b in range(B):
                    pe.wait_ge(xn_ok, 4 * L + b + 1)
                    for j in range(HN):
                        n = HN * b + j
                        if n >= 3:
                            pe.wait_ge(h_ok, NU * L + n - 2)
                        s = slots[n % 3]
                        m = 128 if j < HT else TAIL
                        mm(s[0:m, 0:512], w1_sb[:, 128 * j:128 * j + m], xn[:, S * b:S * b + S])
                        mm(s[0:m, 512:1024], w1_sb[:, HID + 128 * j:HID + 128 * j + m], xn[:, S * b:S * b + S]).then_inc(h_mm, 1)
                        if j == 1 and b:
                            down(b - 1)
                down(B - 1)

            for n in range(NT):
                pe.wait_ge(f_p, n // 4 + 1)
                i = pe.transpose(X[:, 128 * n:128 * n + 128], fin[:, 128 * n:128 * n + 128], ident)
                if n % 4 == 3:
                    i.then_inc(f_tr, 1)


        @block.scalar
        def _(act):
            def copy(o, i):
                return act.activation(o, i, ACT.Copy)

            act.sem_inc(o_ev, 8)
            act.sem_inc(a_out, 1)
            for q in range(4):
                act.wait_ge(i_tr, 4 * q + 4)
                copy(xT[:, S * q:S * q + S], bank(Y, q)).then_inc(i_xT, 1)

            act.wait_ge(ld_w0, 96)
            act.wait_ge(init_p, 9)

            def l0_latent(b):
                act.wait_ge(a_lat, b + 1)
                act.activation(latA[0:LAT, :], bank(Y, 1)[0:LAT], ACT.Identity,
                               bias=vec0_sb[0:LAT, 3:4]).then_inc(a_latA, 1)

            def l0_exps(b):
                for lot in range(8):
                    if lot >= 3:
                        act.wait_ge(a_pv, 8 * b + lot - 2)
                    for c in range(4):
                        n = 4 * lot + c
                        act.wait_ge(a_sT, 32 * b + n + 65)
                        act.activation(PT[lot % 3][:, c], bank(X, 2 * (n % 2), 2).rearrange("p (k t) -> p k t", k=2),
                                       ACT.Exp).then_inc(a_exp, 1)
                act.wait_ge(a_acc, b + 1)
                act.activation(s_new[:, ds(b * S, S)], bank(Y, 3), ACT.Identity, bias=vec0_sb[:, 2:3]).then_inc(a_out, 1)

            l0_latent(0)
            with act.Fori(0, B - 1) as b:
                l0_latent(b + 1)
                l0_exps(b)
            l0_exps(B - 1)

            def project(it, t, ns=range(4), first=False):
                if not first and ns[0] == 0:
                    act.wait_ge(u_ok, 2 * it + t - 1)
                    act.wait_ge(c_ok, 2 * it + t - 1)
                for n in ns:
                    b = (1, 2, 3, 0)[n]
                    act.wait_ge(p_mm, 8 * it + 4 * t + n + 1)
                    copy((qE, kE)[t][:, S * b:S * b + S], bank(Y, b)).then_inc(p_ev, 1)

            def squares(it):
                for t in range(2):
                    act.wait_ge(p_ev, 8 * it + 4 * t + 4)
                    act.activation((sqq, sqk)[t], (qE, kE)[t], ACT.Square).then_inc(sq_ok, 1)

            def diagonal(it, par, bs):
                act.wait_ge(pn_ok, 2 * it + 2)
                act.wait_ge(o_mm, 4 * it + 1)
                for b in bs:
                    r = slice(32 * b, 32 * b + 32)
                    copy(PD[r, :, :, :, b, :].rearrange("p h w s l -> p (h w s) l"),
                         P[par][r].rearrange("p (n l) -> p n l", l=W)).then_inc(pd_ok, 1)

            def project_v(it, par):
                for c in range(4):
                    act.wait_ge(v_mm, 4 * it + c + 1)
                    copy(V[par][:, 4 * c:4 * c + 4, :], bank(Y, c).rearrange("p (w c) -> p w c", c=128)).then_inc(v_ev, 1)

            def exps(it, par, h):
                act.wait_ge(s_sub, 2 * it + h + 1)
                Ph = P[par][:, 1024 * h:1024 * h + 1024]
                act.activation(Ph, Ph, ACT.Exp).then_inc(e_ok, 1)

            def outputs(it):
                for n in range(4):
                    act.wait_ge(o_mm, 4 * it + n + 2)
                    copy(oT[:, S * n:S * n + S], bank(X, n)).then_inc(o_ev, 1)

            def first_step(it):
                project(it + 1, 0)
                project(it + 1, 1)
                squares(it + 1)
                exps(it, 0, 0)
                project_v(it + 1, 1)
                exps(it, 0, 1)
                diagonal(it, 0, (0, 1))

            def step(it, par):
                project(it + 1, 0)
                diagonal(it - 1, 1 - par, (2, 3))
                project(it + 1, 1, (0,))
                exps(it, par, 0)
                project(it + 1, 1, (1, 2, 3))
                exps(it, par, 1)
                squares(it + 1)
                outputs(it - 1)
                project_v(it + 1, 1 - par)
                diagonal(it, par, (0, 1))

            with act.Fori(0, DEPTH) as L:
                act.wait_ge(z_add, 4 * L + 4)
                copy(xs[0:64, :, :], xT[0:64].rearrange("p (b t) -> p b t", b=B)).then_inc(xs_ok, 1)
                act.wait_ge(par_ok, L + 1)
                project(L * PAIRS, 0, first=True)
                project(L * PAIRS, 1, first=True)
                squares(L * PAIRS)
                project_v(L * PAIRS, 0)
                first_step(L * PAIRS)
                with act.Fori(0, PAIRS // 2 - 1) as j:
                    for k in range(2):
                        step(L * PAIRS + j * 2 + k + 1, 1 - k)
                it = L * PAIRS + PAIRS - 1
                diagonal(it - 1, 0, (2, 3))
                exps(it, 1, 0)
                exps(it, 1, 1)
                outputs(it - 1)
                diagonal(it, 1, (0, 1))
                outputs(it)

                act.wait_ge(y_add, 4 * PAIRS * L + 4 * PAIRS + 12)
                copy(xs[0:64, :, :], xT[0:64].rearrange("p (b t) -> p b t", b=B)).then_inc(xs_ok, 1)
                for b in range(B):
                    act.wait_ge(c_mm, 4 * L + b + 1)
                    act.activation(xsq[:, S * b:S * b + S], bank(Y, b), ACT.Square)
                    act.activation(xc[:, S * b:S * b + S], bank(Y, b), ACT.Identity,
                                   scale=par_sb[:, 2:3]).then_inc(c_ev, 1)
                for b in range(B):
                    act.wait_ge(t_ok, 4 * L + b + 1)
                    act.activation(xn[:, S * b:S * b + S], xn[:, S * b:S * b + S], ACT.Identity,
                                   bias=par_sb[:, 3:4]).then_inc(xn_ok, 1)
                slots = (bank(X, 0, 2), bank(X, 2, 2), bank(Y, 0, 2))
                for n in range(NU):
                    j = n % HN
                    act.wait_ge(h_mm, NU * L + n + 1)
                    if n >= 4:
                        act.wait_ge(h_ok, NU * L + n - 3)
                    m = 128 if j < HT else TAIL
                    act.activation(gel[0:m, n % 4, :], slots[n % 3][0:m, 512:1024], ACT.Gelu,
                                   bias=par_sb[0:m, 5 + HN + j:6 + HN + j]).then_inc(g_ok, 1)

            for b in range(B):
                if b == 0:
                    act.wait_ge(z_add, 4 * DEPTH + 4)
                act.activation(gate[:, S * b:S * b + S], xT[:, S * b:S * b + S], ACT.Silu).then_inc(f_g, 1)

        @block.vector
        def _(v):
            steps = [0]

            def link(ins, s, base):
                steps[0] += 1
                ins.then_inc(s, 1)
                v.wait_ge(s, base + steps[0])

            def bcast(a, n):
                return a.unsqueeze(2).broadcast_to([128, a.shape[1], n])

            def inverse_root(r, a, t, s, base):
                i32 = mybir.dt.int32
                link(v.tensor_scalar(r.bitcast(i32), a.bitcast(i32), -0.5, float(0x5F3759DF), ALU.mult, ALU.add), s, base)
                for _ in range(4):
                    link(v.tensor_tensor(t, r, r, ALU.mult), s, base)
                    link(v.scalar_tensor_tensor(t, t, -0.5, a, ALU.mult, ALU.mult), s, base)
                    link(v.scalar_tensor_tensor(r, t, 1.5, r, ALU.add, ALU.mult), s, base)

            v.sem_inc(y_add, 12)
            v.sem_inc(z_add, 4)
            v.wait_ge(ld_c, 48)
            v.tensor_copy(identb[:], ident).then_inc(init_v, 1)
            v.tensor_copy(mask_sb[:], mask_f).then_inc(init_v, 1)
            v.memset(red[:], NEG).then_inc(init_v, 1)
            v.memset(rsum[:], 0.0).then_inc(init_v, 1)
            v.memset(mx_row[:], 0.0).then_inc(init_v, 1)
            v.memset(dn_row[:], 1.0).then_inc(init_v, 1)
            v.memset(rq_row[:], 1.0).then_inc(init_v, 1)
            for n in range(NT):
                if n % 4 == 0:
                    v.wait_ge(ld_x[n // 4], 16)
                v.bn_stats(st6[:, n, :], x_in[:, n, :]).then_inc(i_var, 1)
            for n in range(NT):
                v.wait_ge(i_var, n + 1)
                v.bn_aggr(mv[:, n, :], st6[:, n, :]).then_inc(dv, 1)
            v.wait_ge(dv, NT)
            steps[0] = 0
            link(v.tensor_scalar(var0[:], mv[:, :, 1], 1e-5, None, ALU.add), dv, NT)
            inverse_root(rstd0[:], var0[:], var0t[:], dv, NT)
            for n in range(NT):
                v.tensor_scalar(x_n[:, n, :], x_in[:, n, :], mv[:, n, 0:1], rstd0[:, n:n + 1],
                                ALU.subtract, ALU.mult).then_inc(i_xn, 1)

            v.wait_ge(ld_w0, 96)

            def split(t, src, base):
                for c in range(3):
                    link(v.tensor_copy(pieces[:, t, c, :], src), lo, base)
                    if c < 2:
                        link(v.tensor_tensor(src, src, pieces[:, t, c, :], ALU.subtract), lo, base)

            def l0_qk(b):
                steps[0], base = 0, 17 * b
                v.wait_ge(a_q, b + 1)
                link(v.tensor_scalar(qf, bank(Y, 0), vec0_sb[:, 0:1], float(DH) ** -0.5, ALU.add, ALU.mult), lo, base)
                v.sem_inc(a_qf, 1)
                split(0, qf, base)
                v.sem_inc(a_pc, 1)
                v.wait_ge(a_k, b + 1)
                link(v.tensor_scalar(kf, bank(Y, 0), vec0_sb[:, 1:2], None, ALU.add), lo, base)
                v.sem_inc(a_kf, 1)
                split(1, kf, base)
                v.sem_inc(a_pc, 1)

            def l0_v(b):
                v.wait_ge(a_vmm, b + 1)
                v.tensor_copy(V32[:, :, :, 0:DH], bank(Y, 2).rearrange("p (k h c) -> p k h c", k=4, c=DH)).then_inc(a_v, 1)

            def l0_top(b, ns):
                for n in ns:
                    v.wait_ge(a_s, 64 * b + n + 1)
                    v.tensor_reduce(mx0[:, n // 4, n % 4:n % 4 + 1], bank(Y, n % 2), AX.X, ALU.max).then_inc(a_mx, 1)

            def l0_top2(b, ms, first):
                for m in ms:
                    n = 2 * m
                    v.wait_ge(a_s, 64 * b + n + 2)
                    v.tensor_reduce(mx0[:, n // 4, n % 4:n % 4 + 2], top_slots[(m - first) % 3].rearrange("p (q t) -> p q t", q=2),
                                    AX.X, ALU.max).then_inc(a_mx, 2)

            def l0_rows(b):
                base = 17 * b
                v.wait_ge(a_mx, 64 * b + 64)
                link(v.tensor_scalar(mneg[:], mx0[:].rearrange("p h q -> p q h"), -1.0, None, ALU.mult), lo, base)
                for c in range(3):
                    i = v.tensor_copy(mpc[:, :, c, :], mneg[:])
                    if c < 2:
                        link(i, lo, base)
                        link(v.tensor_tensor(mneg[:], mneg[:], mpc[:, :, c, :], ALU.subtract), lo, base)
                    else:
                        i.then_inc(a_mp, 1)
                assert steps[0] == 17, steps
                v.wait_ge(a_mt, b + 1)
                v.tensor_copy(mrows[:], bank(Y, 0).bitcast(bf16)[0:48, 0:512]).then_inc(a_mr, 1)

            def l0_group(b, g):
                v.wait_ge(a_pv, 8 * b + 2 * g + 2)
                if g:
                    v.wait_ge(a_on, 4 * b + g)
                v.tensor_copy(raw, bank(Y, 2)).then_inc(a_raw, 1)
                v.wait_ge(a_raw, 4 * b + g + 1)
                v.transpose(rawT[:].rearrange("p w c -> p (w c)"), raw).then_inc(a_rT, 1)
                v.wait_ge(a_rT, 4 * b + g + 1)
                v.reciprocal(rq0[:], rawT[:, :, DH]).then_inc(a_den, 1)
                v.wait_ge(a_den, 4 * b + g + 1)
                v.transpose(rden.rearrange("p (w c) -> p w c", c=32), bcast(rq0[:], 32)).then_inc(a_rec, 1)

            def l0_step(b):
                l0_qk(b + 1)
                l0_group(b, 0)
                l0_group(b, 1)
                l0_top(b + 1, range(0, 28 - BESIDE))
                l0_group(b, 2)
                l0_top(b + 1, range(28 - BESIDE, AHEAD))
                l0_group(b, 3)
                l0_top2(b + 1, range(AHEAD // 2, 22), AHEAD // 2)
                l0_v(b + 1)
                l0_top2(b + 1, range(22, 32), AHEAD // 2)
                l0_rows(b + 1)

            l0_qk(0)
            l0_v(0)
            l0_top2(0, range(32), 0)
            l0_rows(0)
            with v.Fori(0, B - 1) as b:
                l0_step(b)
            for g in range(4):
                l0_group(B - 1, g)

            def softmax_top(it, par, h):
                Ph = P[par][:, 1024 * h:1024 * h + 1024]
                v.wait_ge(s_mm, 2 * it + h + 1 + 2)
                v.wait_ge(m_ok, 2 * it + h + 1)
                v.tensor_tensor(Ph, X[:, 1024 * h:1024 * h + 1024], Ph, ALU.mult).then_inc(s_rd, 1)
                v.wait_ge(s_rd, 2 * it + h + 1)
                base = 12 * it
                link(v.tensor_reduce(skew(red, h), Ph.rearrange("p (n c) -> p n c", c=32), AX.X, ALU.max,
                                     apply_transpose=True), sm, base)
                link(v.tensor_tensor(mx[:, h, :], red[:, h, 0:NW], red[:, h, NW + 1:2 * NW + 1], ALU.max), sm, base)
                link(v.transpose(mx_row[:, h, 0:NW, :], bcast(mx[:, h, :], 32)), sm, base)
                v.tensor_tensor(Pv[par][:, h], Pv[par][:, h], pairs(mx_row, h), ALU.subtract).then_inc(s_sub, 1)

            def softmax_sums(it, par, h):
                base = 12 * it
                v.wait_ge(e_ok, 2 * it + h + 1)
                link(v.tensor_reduce(skew(rsum, h), P[par][:, 1024 * h:1024 * h + 1024].rearrange("p (n c) -> p n c", c=32),
                                     AX.X, ALU.add, apply_transpose=True), sm, base)
                link(v.tensor_tensor(dn[:, h, :], rsum[:, h, 0:NW], rsum[:, h, NW + 1:2 * NW + 1], ALU.add), sm, base)
                link(v.reciprocal(rd[:, h, :], dn[:, h, :]), sm, base)
                v.transpose(dn_row[:, h, 0:NW, :], bcast(rd[:, h, :], 32)).then_inc(d_ok, 1)

            def skew(t, h):
                return t[:, h, :].rearrange("p (s k) -> p k s", s=2)[:, 0:NW, :]

            SWAP = [(i + 16) % 32 for i in range(32)]

            def cos_part(it, t):
                v.wait_ge(p_ev, 8 * it + 4 * t + 4)
                v.wait_ge(s_mm, 2 * it + 2)
                v.tensor_tensor((qr, kr)[t].rearrange("p (b t) -> p b t", b=B),
                                (qE, kE)[t].rearrange("p (b t) -> p b t", b=B),
                                rot_sb[:, 2 * t:2 * t + 1, :].broadcast_to([128, B, S]), ALU.mult).then_inc(c_ok, 1)

            def sin_part(it, t):
                v.wait_ge(u_ok, 2 * it + t + 1)
                stand(v)
                v.stream_shuffle((uq, uk)[t], (uq, uk)[t], SWAP).then_inc(sh_ok, 1)

            def norms_read(it):
                v.wait_ge(ss_mm, it + 1)
                v.transpose(ss_t[:].rearrange("p w c -> p (w c)"), bank(Y, 0)).then_inc(ss_tr, 1)

            def norms(it):
                v.wait_ge(ss_tr, it + 1)
                c, base, steps[0] = steps[0], 14 * it, 0
                link(v.tensor_scalar(ssg[:], ss_t[:, :, 0:4].rearrange("p w c -> p c w"), 1e-24, None, ALU.max), rs, base)
                flat = "p c w -> p (c w)"
                inverse_root(rn[:].rearrange(flat), ssg[:].rearrange(flat), ssw[:], rs, base)
                assert steps[0] == 14
                steps[0] = c
                for h in range(2):
                    v.transpose(rq_row[:, h, 0:NW, :], bcast(rn[:, h, :], 32)).then_inc(rq_ok, 1)

            xw = xT[:, :].rearrange("p (b w l) -> p w b l", b=B, l=W)

            def add_y(it):
                for n, b in enumerate((1, 2, 3, 0)):
                    v.wait_ge(y_mm, 4 * it + n + 1)
                    v.wait_ge(y_add, 4 * it + n + 9)
                    v.tensor_tensor(xw[:, 4 * n:4 * n + 4], bank(Y, b).rearrange("p (w b l) -> p w b l", w=4, b=B),
                                    xw[:, 4 * n:4 * n + 4], ALU.add).then_inc(y_add, 1)

            def first_step(it):
                steps[0] = 0
                softmax_top(it, 0, 0)
                cos_part(it + 1, 0)
                sin_part(it + 1, 0)
                cos_part(it + 1, 1)
                sin_part(it + 1, 1)
                norms_read(it + 1)
                norms(it + 1)
                softmax_top(it, 0, 1)
                softmax_sums(it, 0, 0)
                softmax_sums(it, 0, 1)
                assert steps[0] == 12

            def step(it, par):
                steps[0] = 0
                softmax_top(it, par, 0)
                softmax_top(it, par, 1)
                cos_part(it + 1, 0)
                softmax_sums(it, par, 0)
                sin_part(it + 1, 0)
                softmax_sums(it, par, 1)
                cos_part(it + 1, 1)
                sin_part(it + 1, 1)
                norms_read(it + 1)
                add_y(it - 1)
                norms(it + 1)
                assert steps[0] == 12

            v.wait_ge(ld_c, 48)
            v.wait_ge(xs_zero, 1)
            v.wait_ge(i_xT, 4)
            v.wait_ge(a_out, B + 1)
            x4 = xT[:, :].rearrange("p (b t) -> p b t", b=B)
            with v.Fori(0, DEPTH) as L:
                v.wait_ge(z_add, 4 * L + 4)
                v.tensor_copy(par_sb[:], par_all[:, ds(L * NPAR, NPAR)]).then_inc(par_ok, 1)
                v.tensor_copy(xs[64:128, :, 1:S], x4[64:128, :, 0:S - 1]).then_inc(xs_ok, 1)
                v.wait_ge(par_ok, L + 1)
                v.wait_ge(ld_rot, 16 * L + 16)
                for t in range(2):
                    r = rot_sb[:, 2 * t:2 * t + 2, :]
                    v.tensor_scalar(r, r, par_sb[:, t:t + 1], None, ALU.mult).then_inc(rot_ok, 1)
                v.wait_ge(xs_ok, 4 * L + 2)
                v.tensor_copy(xsw.rearrange("p w (b l) -> p w b l", b=B),
                              xs[:].rearrange("p b (w l) -> p w b l", w=NW)).then_inc(xsw_ok, 1)
                v.wait_ge(rot_ok, 2 * L + 2)
                cos_part(L * PAIRS, 0)
                sin_part(L * PAIRS, 0)
                cos_part(L * PAIRS, 1)
                sin_part(L * PAIRS, 1)
                norms_read(L * PAIRS)
                norms(L * PAIRS)
                first_step(L * PAIRS)
                with v.Fori(0, PAIRS // 2 - 1) as j:
                    for k in range(2):
                        step(L * PAIRS + j * 2 + k + 1, 1 - k)
                steps[0] = 0
                it = L * PAIRS + PAIRS - 1
                softmax_top(it, 1, 0)
                softmax_top(it, 1, 1)
                softmax_sums(it, 1, 0)
                softmax_sums(it, 1, 1)
                v.wait_ge(pn_ok, 2 * it + 2)
                v.wait_ge(o_mm, 4 * it + 1)
                for b in (2, 3):
                    r = slice(32 * b, 32 * b + 32)
                    v.tensor_copy(PD[r, :, :, :, b, :].rearrange("p h w s l -> p (h w s) l"),
                                  P[1][r].rearrange("p (n l) -> p n l", l=W)).then_inc(pd_ok, 1)
                add_y(it - 1)
                add_y(it)

                v.wait_ge(y_add, 4 * PAIRS * L + 4 * PAIRS + 12)
                v.tensor_copy(xs[64:128, :, 1:S], x4[64:128, :, 0:S - 1]).then_inc(xs_ok, 1)
                v.wait_ge(var_mm, L + 1)
                steps[0] = 0
                base = 15 * L
                link(v.transpose(varw[:].rearrange("p w c -> p (w c)"), bank(X, 0)), vr, base)
                link(v.tensor_scalar(var0[:], varw[:, :, 0], 1e-5, None, ALU.add), vr, base)
                inverse_root(rstd0[:], var0[:], var0t[:], vr, base)
                v.transpose(rstd_sb.rearrange("p (w c) -> p w c", c=32), bcast(rstd0[:], 32)).then_inc(rs_ok, 1)
                assert steps[0] == 15
                for b in range(B):
                    v.wait_ge(rb_mm, 4 * L + b + 1)
                    v.tensor_tensor(xn[:, S * b:S * b + S], bank(Y, b), xc[:, S * b:S * b + S], ALU.mult).then_inc(t_ok, 1)
                slots = (bank(X, 0, 2), bank(X, 2, 2), bank(Y, 0, 2))

                def add_z(b):
                    v.wait_ge(z_mm, 4 * L + b + 1)
                    v.scalar_tensor_tensor(xT[:, S * b:S * b + S], bank(Y, 2 + b % 2), par_sb[:, 4:5],
                                           xT[:, S * b:S * b + S], ALU.add, ALU.add).then_inc(z_add, 1)

                for b in range(B):
                    for j in range(HN):
                        n = HN * b + j
                        v.wait_ge(g_ok, NU * L + n + 1)
                        if j == 0 and b >= 2:
                            v.wait_ge(z_mm, 4 * L + b - 1)
                        m = 128 if j < HT else TAIL
                        v.scalar_tensor_tensor(hid[0:m, b % 2, j, :], slots[n % 3][0:m, 0:512], par_sb[0:m, 5 + j:6 + j],
                                               gel[0:m, n % 4, :], ALU.add, ALU.mult).then_inc(h_ok, 1)
                        if j == HN - 1 and b:
                            add_z(b - 1)
                add_z(B - 1)

            v.wait_ge(ld_end, 32)
            for b in range(B):
                v.wait_ge(f_g, b + 1)
                v.tensor_tensor(fin[:, S * b:S * b + S], sT[:, S * b:S * b + S], gate[:, S * b:S * b + S], ALU.mult).then_inc(f_p, 1)
            for q in range(4):
                v.wait_ge(f_tr, q + 1)
                v.tensor_tensor(x_tok[:, 4 * q:4 * q + 4, :], bank(X, q).rearrange("p (n d) -> p n d", d=D),
                                x_tok[:, 4 * q:4 * q + 4, :], ALU.add).then_inc(f_o, 1)

        @block.gpsimd
        def _(pool):
            n = 0

            def fill(a, value):
                nonlocal n
                pool.memset(a, value).then_inc(init_p, 1)
                n += 1
                pool.wait_ge(init_p, n)

            for p in range(2):
                fill(qst[p][64:96, :, :], 0.0)
                fill(kst[p][64:96, :, :], 0.0)
                fill(kst[p][96:99, :, :], 1.0)
                if p == 0:
                    fill(latA[32:64, :], 1.0)
                    fill(V32[:, :, :, DH:32], 1.0)
            fill(xs[64:128, :, 0:1], 0.0)
            pool.sem_inc(xs_zero, 1)
            pool.wait_ge(init_v, 7)
            with pool.Fori(0, B) as b:
                for g in range(4):
                    pool.wait_ge(a_rec, 4 * b + g + 1)
                    pool.tensor_tensor(onorm[:, g, :], raw, rden, ALU.mult).then_inc(a_on, 1)

            def sin_part(it, t):
                pool.wait_ge(p_ev, 8 * it + 4 * t + 4)
                pool.tensor_tensor((uq, uk)[t].rearrange("p (b t) -> p b t", b=B),
                                   (qE, kE)[t].rearrange("p (b t) -> p b t", b=B),
                                   rot_sb[:, 2 * t + 1:2 * t + 2, :].broadcast_to([128, B, S]), ALU.mult).then_inc(u_ok, 1)

            def join(it, t):
                pool.wait_ge(c_ok, 2 * it + t + 1)
                pool.wait_ge(sh_ok, 2 * it + t + 1)
                pool.tensor_tensor((qr, kr)[t], (qr, kr)[t], (uq, uk)[t], ALU.add).then_inc(r_ok, 1)

            def norms(it, par):
                pool.wait_ge(rs, 14 * it + 14)
                stand(pool)
                pool.tensor_scalar(rk8[:], rn[:, 2:4, :], 8.0, None, ALU.mult).then_inc(po, 1)
                pool.wait_ge(po, it + 1)
                for h in range(2):
                    pool.wait_ge(rq_ok, 2 * it + h + 1)
                    pool.tensor_tensor(Pv[par][:, h], rk8[:, h, :].unsqueeze(2).broadcast_to([128, NW, 64]),
                                       pairs(rq_row, h), ALU.mult).then_inc(m_ok, 1)

            def normalise(it, par, h):
                pool.wait_ge(d_ok, 2 * it + h + 1)
                pool.tensor_tensor(Pv[par][:, h], Pv[par][:, h], pairs(dn_row, h), ALU.mult).then_inc(pn_ok, 1)

            def first_step(it):
                sin_part(it + 1, 0)
                sin_part(it + 1, 1)
                join(it + 1, 0)
                join(it + 1, 1)
                norms(it + 1, 1)
                normalise(it, 0, 0)
                normalise(it, 0, 1)

            def step(it, par):
                sin_part(it + 1, 0)
                sin_part(it + 1, 1)
                normalise(it, par, 0)
                join(it + 1, 0)
                normalise(it, par, 1)
                join(it + 1, 1)
                pool.wait_ge(pd_ok, 4 * it)
                norms(it + 1, 1 - par)

            pool.wait_ge(a_out, B + 1)
            pool.wait_ge(s_saved, 16)
            pool.memset(region(14, 4), 0.0).then_inc(pd_zero, 1)
            pool.wait_ge(pd_zero, 1)
            with pool.Fori(0, DEPTH) as L:
                pool.wait_ge(rot_ok, 2 * L + 2)
                sin_part(L * PAIRS, 0)
                sin_part(L * PAIRS, 1)
                join(L * PAIRS, 0)
                join(L * PAIRS, 1)
                norms(L * PAIRS, 0)
                first_step(L * PAIRS)
                with pool.Fori(0, PAIRS // 2 - 1) as j:
                    for k in range(2):
                        step(L * PAIRS + j * 2 + k + 1, 1 - k)
                it = L * PAIRS + PAIRS - 1
                normalise(it, 1, 0)
                normalise(it, 1, 1)


def _constants():
    f = np.float32
    half = np.arange(0, HD, 2, dtype=f)
    inv = (1.0 / f(10000.0) ** (half / f(HD))).astype(f)
    t = np.arange(S, dtype=f)
    fr = (t[:, None] * inv[None, :]).astype(f)
    base = ((half + f(0.4 * HD)) / f(1.4 * HD)).astype(f)
    sc = (base[None, :] ** ((t - f(S // 2)) / f(W // 2))[:, None]).astype(f)
    cos, sin = np.cos(fr), np.sin(fr)
    e = np.arange(16)
    idx = np.concatenate([np.concatenate([16 * g + e, 16 * g + e]) for g in range(2)])
    sign = np.concatenate([np.concatenate([np.ones(16), -np.ones(16)]) for g in range(2)])
    idx, sign = np.tile(idx, 2), np.tile(sign, 2).astype(f)
    rot = []
    for s in (sc, (1.0 / sc).astype(f)):
        rot.append((cos * s)[:, idx].T)
        rot.append((sin * s)[:, idx].T * sign[:, None])
    rot = np.concatenate(rot, axis=1).astype(f)
    j, i = np.arange(W)[:, None], np.arange(W)[None, :]
    own = np.where(j <= i, 0.0, NEG)
    nxt = np.where(j >= i, 0.0, NEG)
    m = np.tile(np.concatenate([own, nxt], axis=1), (1, NW))
    m[:, -W:] = NEG
    mask = np.tile(m, (4, 1)).astype(f)
    const = np.zeros((128, 608), f)
    const[:, 0:128] = np.eye(128)
    const[:, 128:256] = np.eye(128) - 1.0 / 128
    for q in range(4):
        const[32 * q, 256:384] = 1.0
        const[32 * q + DH, 384 + 32 * q:384 + 32 * q + 32] = 1.0
    for a in range(2):
        for h in range(2):
            const[64 * h:64 * h + 64, 512 + 32 * a + 2 * a + h] = 1.0
    const[:, 576:608] = 1.0 / 128
    return rot, mask, const


def _layout(i):
    f = np.float32
    g = {k: np.asarray(v) for k, v in i.items()}
    rh = lambda a: np.ascontiguousarray(a.reshape(-1, H, DH).transpose(0, 2, 1).reshape(-1, D))
    vec = np.zeros((128, 4), f)
    vec[:, 0], vec[:, 1] = rh(g["L0_attn_bq"][None])[0], rh(g["L0_attn_bk"][None])[0]
    vec[:, 2], vec[:LAT, 3] = g["L0_attn_bo"], g["L0_attn_bl"]
    wog = np.zeros((128, 4, 128), f)
    for h in range(H):
        wog[32 * (h % 4):32 * (h % 4) + DH, h // 4] = g["L0_attn_Wo"][DH * h:DH * h + DH]
    e = np.arange(16)
    order = np.concatenate([np.concatenate([16 * q + e, 32 + 16 * q + e]) for q in range(2)])
    cols = np.concatenate([order, HD + order])
    w = g["L0_ffn_Wqkv"].reshape(DEPTH, D, 3, PAIRS, 128).transpose(0, 3, 1, 2, 4).copy()
    w[..., 0:2, :] = w[..., 0:2, :][..., cols]
    par = np.zeros((DEPTH, 128, NPAR), f)
    par[:, :, 0] = np.tile(g["L0_ffn_q_scale"][:, order], (1, 2))
    par[:, :, 1] = np.tile(g["L0_ffn_k_scale"][:, order], (1, 2))
    par[:, :, 2], par[:, :, 3], par[:, :, 4] = g["L0_ffn_ln_g"], g["L0_ffn_ln_b"], g["L0_ffn_b2"]
    for p, first in ((5, 0), (5 + HN, HID)):
        b = g["L0_ffn_b1"][:, first:first + HID]
        par[:, :, p:p + HT] = b[:, :HT * 128].reshape(DEPTH, HT, 128).transpose(0, 2, 1)
        par[:, :TAIL, p + HT] = b[:, HT * 128:]
    rot, mask, const = _constants()
    return dict(
        x=g["L0_attn_x"].reshape(T, D), wq0=rh(g["L0_attn_Wq"]), wl0=g["L0_attn_Wl"], wk0=rh(g["L0_attn_Wk"]),
        wv0=np.concatenate([g["L0_attn_Wv"], g["L0_attn_bv"][None]]), vec0=vec, wog0=wog.reshape(128, 512),
        qkv=w.reshape(DEPTH * PAIRS, D, 3, 128), wo=g["L0_ffn_Wo"].reshape(DEPTH * PAIRS, 128, D),
        par=par.transpose(1, 0, 2).reshape(128, DEPTH * NPAR), w1=g["L0_ffn_W1"], w2=g["L0_ffn_W2"],
        rot=rot, mask=mask, const=const)


def kernel(**inputs):
    import concourse.bacc as bacc
    from concourse.bass_utils import run_bass_kernel_spmd

    nc = bacc.Bacc("TRN2", target_bir_lowering=False, num_devices=1)
    arrays = {k: np.ascontiguousarray(a) for k, a in _layout(inputs).items()}
    args = {k: nc.dram_tensor(k, a.shape, mybir.dt.from_np(a.dtype), kind="ExternalInput").ap() for k, a in arrays.items()}
    out = nc.dram_tensor("out", (T, D), mybir.dt.float32, kind="ExternalOutput").ap()
    gated_stack_kernel(nc, **args, out=out)
    r = run_bass_kernel_spmd(nc, [arrays], core_ids=[0])
    return r.results[0]["out"].reshape(B, S, D)
```
